# Optimizing a Trainium2 kernel written in Bass

```python
import numpy as np
import jax
import jax.numpy as jnp

def _softmax(x, axis=-1):
    return jax.nn.softmax(x, axis=axis)

def _gelu(x):
    return jax.nn.gelu(x, approximate=True)

def _silu(x):
    return jax.nn.silu(x)

def _sigmoid(x):
    return jax.nn.sigmoid(x)

def _layernorm(x, axis=-1, eps=1e-05):
    m = jnp.mean(x, axis=axis, keepdims=True)
    v = jnp.var(x, axis=axis, keepdims=True)
    return (x - m) / jnp.sqrt(v + eps)

def _scatter_add(tgt, idx, src, axis=0):
    return tgt.at[idx].add(src)

def _segment_sum(src, seg, n):
    return jax.ops.segment_sum(src, seg, n)
kernel_name = 'mk_adj_preln_d2_adj_r2_2d683a'

def setup_inputs(seed: int=0):
    np.random.seed(seed)
    _w = jnp.asarray

    def _rec_inputs():
        import jax
        import jax.numpy as jnp
        _gk = jax.random.key(seed)
        x = -0.000929 + 1 * jax.random.normal(jax.random.fold_in(_gk, 1), (4096, 128), jnp.float32)
        _a = jax.random.bernoulli(jax.random.fold_in(_gk, 2), 0.00390625, (4096, 4096))
        adj = _a.astype(jnp.int32)
        return (x, adj)
    x, adj = _rec_inputs()

    def _L0_gnn_setup():
        import jax
        import jax.numpy as jnp
        import numpy as np
        from jax import lax
        N = 4096
        F = 128
        CHUNK = 64
        key = jax.random.key(seed)
        kx, ka = jax.random.split(key)
        X = jax.random.normal(kx, (N, F), dtype=jnp.float32)
        adj = jax.random.randint(ka, (N, N), 0, 2, dtype=jnp.int32)
        return {'X': X, 'adj': adj}
    _L0_gnn_all = _L0_gnn_setup()
    _L0_gnn_in = {k: v for k, v in _L0_gnn_all.items() if k in ()}
    del _L0_gnn_all

    def _L1_gnn_setup():
        import jax, jax.numpy as jnp
        import numpy as np
        NEG_INF = -9000000000000000.0
        ALPHA = 0.2
        key = jax.random.key(seed)
        k1, k2, k3, k4 = jax.random.split(key, 4)
        N, F_IN, H, D = (4096, 128, 4, 32)
        h = jax.random.normal(k1, (N, F_IN), dtype=jnp.float32)
        adj = jax.random.randint(k2, (N, N), 0, 2, dtype=jnp.int32)
        W = jax.random.normal(k3, (F_IN, H * D), dtype=jnp.float32) * (1.0 / np.sqrt(F_IN))
        a = jax.random.normal(k4, (1, H, 2 * D), dtype=jnp.float32)
        return {'h': h, 'adj': adj, 'W': W, 'a': a}
    _L1_gnn_all = _L1_gnn_setup()
    _L1_gnn_in = {k: v for k, v in _L1_gnn_all.items() if k in ('W', 'a')}
    del _L1_gnn_all
    return {'x': x, 'adj': adj, 'L1_gnn_W': _L1_gnn_in['W'], 'L1_gnn_a': _L1_gnn_in['a']}

def reference(x, adj, L1_gnn_W, L1_gnn_a):
    import jax
    import jax.numpy as jnp

    def _L0_gnn_ref(X, adj):
        import jax
        import jax.numpy as jnp
        import numpy as np
        from jax import lax
        N = 4096
        F = 128
        CHUNK = 64
        neg = jnp.finfo(X.dtype).min
        mask = adj != 0
        n, f = X.shape

        def body(_, mrows):
            vals = jnp.max(jnp.where(mrows[:, :, None], X[None, :, :], neg), axis=1)
            has_nbr = jnp.any(mrows, axis=1)
            return (None, jnp.where(has_nbr[:, None], vals, jnp.zeros((), X.dtype)))
        _, out = lax.scan(body, None, mask.reshape(n // CHUNK, CHUNK, n))
        return out.reshape(n, f)

    def _L1_gnn_ref(h, adj, W, a):
        import jax, jax.numpy as jnp
        import numpy as np
        NEG_INF = -9000000000000000.0
        ALPHA = 0.2
        N = h.shape[0]
        H = a.shape[1]
        D = a.shape[2] // 2
        Wh = (h @ W).reshape(N, H, D)
        a_src = a[0, :, :D]
        a_dst = a[0, :, D:]
        s_src = jnp.einsum('nhd,hd->nh', Wh, a_src)
        s_dst = jnp.einsum('nhd,hd->nh', Wh, a_dst)
        e = s_src[:, None, :] + s_dst[None, :, :]
        e = jnp.where(e >= 0, e, ALPHA * e)
        e = jnp.where(adj[:, :, None] > 0, e, NEG_INF)
        attention = jax.nn.softmax(e, axis=1)
        h_prime = jnp.einsum('ijh,jhd->ihd', attention, Wh)
        return jax.nn.elu(h_prime.reshape(N, H * D))
    h = jnp.maximum(_layernorm(x, axis=-1), 0.0)
    x = x + _L0_gnn_ref(h, adj)
    h = jnp.maximum(_layernorm(x, axis=-1), 0.0)
    x = x + _L1_gnn_ref(h, adj, L1_gnn_W, L1_gnn_a)
    return x

_drawn_inputs = setup_inputs


def setup_inputs(seed=0):
    import zlib

    import numpy as np

    out = dict(_drawn_inputs(seed))
    spreads = {}
    factors = {}
    for name, (base, spread) in spreads.items():
        noise = np.random.default_rng([zlib.crc32(name.encode()), seed]).standard_normal(out[name].shape)
        drawn = base * np.exp(spread * noise) if base else spread * noise
        out[name] = jnp.asarray(drawn.astype(out[name].dtype))
    for name, factor in factors.items():
        out[name] = (out[name] * factor).astype(out[name].dtype)
    return out
```

```python
import numpy as np
import concourse.bass as bass
from concourse import mybir
from contextlib import ExitStack

F32 = mybir.dt.float32
BF16 = mybir.dt.bfloat16
I32 = mybir.dt.int32
ALU = mybir.AluOpType
ACT = mybir.ActivationFunctionType
AX = mybir.AxisListType

P = 128
ROUNDS = 4
EPS = 1e-5
ALPHA = 0.2
NEG_INF = 9000000000000000.0


def hold(engine, semaphore, value, passed):
    engine.wait_ge(semaphore, value)
    engine.sem_inc(passed, 1)


def emit(nc, x_dram, adj_dram, w_dram, a_dram, out_dram):
    N, F = x_dram.shape
    H, D2 = a_dram.shape[1], a_dram.shape[2]
    D = D2 // 2
    NC = N // P
    GW = 512
    NG = N // GW
    GB = GW // P
    E = F + 2 * H
    adj_chunks = adj_dram.rearrange("(b p) (c j) -> c p b j", p=P, j=P)
    adj_rows = adj_dram.rearrange("(b p) j -> b p j", p=P)
    x_view = x_dram.rearrange("(b p) f -> p b f", p=P)
    out_rows = out_dram.rearrange("(b p) f -> b p f", p=P)

    ctx = ExitStack()

    def sem(name):
        return ctx.enter_context(nc.semaphore(name))

    with ctx:
        def sb(name, shape, dt, where=ctx):
            return where.enter_context(nc.sbuf_tensor(name, shape, dt))

        banks = [ctx.enter_context(nc.psum_tensor(f"bank{i}", [P, 512], F32)) for i in range(8)]

        ident = sb("ident", [P, P], F32)
        xs = sb("xs", [P, NC, F], F32)
        w_ext = sb("w_ext", [P, E], F32)
        acc = sb("acc", [P, N], F32)
        stats = sb("stats", [P, NC, 6], F32)
        mv = sb("mv", [P, NC, 2], F32)
        rstd = sb("rstd", [P, NC], F32)
        epst = sb("epst", [P, 1], F32)

        def layernorm_relu(vec, link, h, sqrt_in_ready, sqrt_done, count):
            for b in range(NC):
                last = nc.vector.bn_stats(stats[:, b, :], xs[:, b, :])
            link(last)
            for b in range(NC):
                last = nc.vector.bn_aggr(mv[:, b, :], stats[:, b, :])
            link(last)
            nc.vector.tensor_scalar(rstd[:], mv[:, :, 1], EPS, None, ALU.add).then_inc(sqrt_in_ready, 1)
            link(nc.vector.tensor_tensor(h[:], xs[:], mv[:, :, 0:1].to_broadcast([P, NC, F]), ALU.subtract))
            vec.wait_ge(sqrt_done, count)
            link(nc.vector.reciprocal(rstd[:], rstd[:]))
            link(nc.vector.tensor_tensor(h[:], h[:], rstd[:].unsqueeze(2).to_broadcast([P, NC, F]), ALU.mult))
            link(nc.vector.tensor_scalar(h[:], h[:], 0.0, None, ALU.max))

        def linker(vec, s):
            count = [0]

            def link(ins):
                count[0] += 1
                ins.then_inc(s, 1)
                vec.wait_ge(s, count[0])
            return link

        first = ExitStack()
        with first:
            ident16 = sb("ident16", [P, P], BF16, first)
            rank_w = sb("rank_w", [P, P], BF16, first)
            hparts = sb("hparts", [P, NC, 3, F], BF16, first)
            adjs = [sb(f"adjs{i}", [P, NC, P], I32, first) for i in range(2)]
            adj_in = [sem(f"adj_in{i}") for i in range(2)]

            scope = ExitStack()
            with scope:
                h = sb("h", [P, NC, F], F32, scope)
                wt = sb("wt", [P, P], F32, scope)
                a_diag = sb("a_diag", [P, 2 * H], F32, scope)
                x_in, w_in, a_in = sem("x_in"), sem("w_in"), sem("a_in")
                vec0, a_zero, ident_built, rank_built = sem("vec0"), sem("a_zero"), sem("ident_built"), sem("rank_built")
                pool0 = sem("pool0")
                var_ready, sqrt_done = sem("var_ready"), sem("sqrt_done")
                wt_ps, wt_sb, wa_ps, wa_sb = sem("wt_ps"), sem("wt_sb"), sem("wa_ps"), sem("wa_sb")

                with nc.Block() as block:
                    @block.sync
                    def _(sp):
                        sp.dma_start(xs[:], x_view).then_inc(x_in, 16)
                        sp.dma_start(w_ext[:, 0:F], w_dram).then_inc(w_in, 16)
                        for s in range(2):
                            sp.dma_start(adjs[s][:], adj_chunks[s]).then_inc(adj_in[s], 16)
                        sp.wait_ge(a_zero, 1)
                        for k in range(2):
                            for hd in range(H):
                                sp.dma_start(a_diag[hd * D:(hd + 1) * D, k * H + hd:k * H + hd + 1],
                                             a_dram[0, hd, k * D:(k + 1) * D].unsqueeze(1)).then_inc(a_in, 16)

                    @block.gpsimd
                    def _(pool):
                        nc.gpsimd.memset(a_diag[:], 0.0).then_inc(a_zero, 1)
                        nc.gpsimd.memset(ident[:], 0.0).then_inc(pool0, 1)
                        nc.gpsimd.memset(rank_w[:], 2.0).then_inc(pool0, 1)
                        pool.wait_ge(pool0, 2)
                        nc.gpsimd.affine_select(out=ident[:], in_=ident[:], compare_op=ALU.not_equal, fill=1.0,
                                                base=0, pattern=[[-1, P]], channel_multiplier=1).then_inc(pool0, 1)
                        nc.gpsimd.affine_select(out=rank_w[:], in_=rank_w[:], compare_op=ALU.is_gt, fill=0.0,
                                                base=0, pattern=[[1, P]], channel_multiplier=-1).then_inc(pool0, 1)
                        pool.wait_ge(pool0, 4)
                        nc.gpsimd.tensor_copy(ident16[:], ident[:]).then_inc(ident_built, 1)
                        pool.wait_ge(ident_built, 1)
                        nc.gpsimd.tensor_tensor(rank_w[:], rank_w[:], ident16[:], ALU.add).then_inc(rank_built, 1)
                        pool.wait_ge(rank_built, 1)

                    @block.scalar
                    def _(act):
                        act.wait_ge(wt_ps, 1)
                        nc.scalar.copy(wt[:], banks[0][:, 0:P]).then_inc(wt_sb, 1)
                        act.wait_ge(wa_ps, 1)
                        nc.scalar.copy(w_ext[:, F:E], banks[1][:, 0:2 * H]).then_inc(wa_sb, 1)
                        act.wait_ge(var_ready, 1)
                        nc.scalar.activation(rstd[:], rstd[:], ACT.Sqrt).then_inc(sqrt_done, 1)
                        act.wait_ge(wa_sb, 1)

                    @block.tensor
                    def _(pe):
                        pe.wait_ge(ident_built, 1)
                        pe.wait_ge(w_in, 16)
                        nc.tensor.transpose(banks[0][:, 0:P], w_ext[:, 0:F], ident[:]).then_inc(wt_ps, 1)
                        pe.wait_ge(wt_sb, 1)
                        pe.wait_ge(a_in, 16 * 2 * H)
                        nc.tensor.matmul(banks[1][:, 0:2 * H], wt[:], a_diag[:], start=True, stop=True).then_inc(wa_ps, 1)

                    @block.vector
                    def _(vec):
                        link = linker(vec, vec0)
                        link(nc.vector.memset(acc[:], 0.0))
                        vec.wait_ge(x_in, 16)
                        layernorm_relu(vec, link, h, var_ready, sqrt_done, 1)
                        for k in range(2):
                            link(nc.vector.tensor_copy(hparts[:, :, k, :], h[:]))
                            if k == 0:
                                link(nc.vector.tensor_tensor(h[:], h[:], hparts[:, :, k, :], ALU.subtract))
                        link(nc.vector.tensor_tensor(hparts[:, :, 2, :], h[:], hparts[:, :, 1, :], ALU.subtract))

            scope = ExitStack()
            with scope:
                adj16 = [sb(f"adj16_{i}", [P, GW], BF16, scope) for i in range(2)]
                mask_t = [sb(f"mask_t{i}", [P, N], BF16, scope) for i in range(2)]
                code = [sb(f"code{i}", [P, N], BF16, scope) for i in range(2)]
                hcur = [sb(f"hcur{i}", [P, 3, F], BF16, scope) for i in range(2)]
                pick = [[sb(f"pick{i}_{r}", [P, GW], BF16, scope) for r in range(ROUNDS)] for i in range(2)]
                opick = [sb(f"opick{g}", [P, GW], BF16, scope) for g in range(NG)]
                last_row = [sb(f"last_row{i}", [P, N // P], BF16, scope) for i in range(2)]
                rowmax = sb("rowmax", [P, 1], F32, scope)
                allmax = sb("allmax", [P, 1], F32, scope)
                top = [sb(f"top{i}", [1, 1], I32, scope) for i in range(2)]
                want = sb("want", [P, 1], F32, scope)

                adj16_ready = sem("adj16_ready")
                turned = sem("turned")
                mask_ready = sem("mask_ready")
                coded = sem("coded")
                code_ready = sem("code_ready")
                hcur_ready = sem("hcur_ready")
                pick_ready = sem("pick_ready")
                gathered = sem("gathered")
                pool_passed, pe_passed, vec_passed = sem("pool_passed"), sem("pe_passed"), sem("vec_passed")
                maxed = sem("maxed")
                chunk_done = sem("chunk_done")
                last_in = [sem(f"last_in{i}") for i in range(2)]
                rowmax_ready, allmax_ready, top_ready = sem("rowmax_ready"), sem("allmax_ready"), sem("top_ready")
                o_pick, o_gathered, o_maxed, want_set = sem("o_pick"), sem("o_gathered"), sem("o_maxed"), sem("want_set")

                turn_ps = [banks[i][:, 0:GW // 2].bitcast(BF16) for i in range(2)]
                code_ps = [banks[2 + i] for i in range(2)]
                gath_ps = [banks[4 + r] for r in range(ROUNDS)]
                chunk = lambda t, s: 2 * t + s

                with nc.Block() as block:
                    @block.sync
                    def _(sp):
                        def serve(c, s, t, load):
                            if load:
                                sp.wait_ge(adj16_ready, NG * (c + 1))
                                sp.dma_start(adjs[s][:], adj_chunks[c + 2]).then_inc(adj_in[s], 16)
                            sp.wait_ge(code_ready, NG * (c + 1))
                            sp.dma_start(last_row[s][:], code[s][P - 1:P, :]
                                         ).then_inc(last_in[s], 16)
                        with sp.Fori(0, NC // 2 - 1) as t:
                            for s in range(2):
                                serve(chunk(t, s), s, t, True)
                        for s in range(2):
                            serve(NC - 2 + s, s, NC // 2 - 1, False)

                    @block.scalar
                    def _(act):
                        def front(c, s, t, g, reuse):
                            u = NG * c + g
                            b = g % 2
                            if g == 0:
                                act.wait_ge(adj_in[s], 16 * (t + 1))
                            if reuse or g >= 2:
                                act.wait_ge(turned, u - 1)
                            nc.scalar.copy(adj16[b][:], adjs[s][:, GB * g:GB * (g + 1), :]).then_inc(adj16_ready, 1)
                            act.wait_ge(turned, u + 1)
                            nc.scalar.copy(mask_t[s][:, g * GW:(g + 1) * GW], turn_ps[b]).then_inc(mask_ready, 1)
                            act.wait_ge(coded, u + 1)
                            if reuse and g == 0:
                                act.wait_ge(chunk_done, c - 1)
                            nc.scalar.copy(code[s][:, g * GW:(g + 1) * GW], code_ps[b][:]).then_inc(code_ready, 1)
                            if g == 0:
                                nc.scalar.copy(hcur[s][:], hparts[:, bass.ts(c, 1), :, :] if not isinstance(c, int)
                                               else hparts[:, c:c + 1, :, :]).then_inc(hcur_ready, 1)

                        for s in range(2):
                            for g in range(NG):
                                front(s, s, 0, g, False)
                        with act.Fori(1, NC // 2) as t:
                            for s in range(2):
                                for g in range(NG):
                                    front(chunk(t, s), s, t, g, True)

                    @block.tensor
                    def _(pe):
                        n_over = pe.alloc_register("pe_over")
                        pe.reg_mov(n_over, 0)

                        def front(c, s, g, reuse):
                            u = NG * c + g
                            b = g % 2
                            pe.wait_ge(adj16_ready, u + 1)
                            if reuse or g >= 2:
                                pe.wait_ge(mask_ready, u - 1)
                            for k in range(GB):
                                last = nc.tensor.transpose(turn_ps[b][:, k * P:(k + 1) * P],
                                                           adj16[b][:, k * P:(k + 1) * P], ident16[:])
                            last.then_inc(turned, 1)
                            pe.wait_ge(mask_ready, u + 1)
                            if reuse or g >= 2:
                                pe.wait_ge(code_ready, u - 1)
                            nc.tensor.matmul(code_ps[b][:], rank_w[:], mask_t[s][:, g * GW:(g + 1) * GW],
                                             start=True, stop=True).then_inc(coded, 1)

                        def gather(c, s, g, reuse):
                            u = NG * c + g
                            if g == 0:
                                pe.wait_ge(hcur_ready, c + 1)
                            for r in range(ROUNDS):
                                pe.wait_ge(pick_ready, ROUNDS * u + r + 1)
                                if reuse or g >= 1:
                                    pe.wait_ge(maxed, ROUNDS * (u - 1) + r + 1)
                                for k in range(3):
                                    last = nc.tensor.matmul(gath_ps[r][:], hcur[s][:, k, :], pick[g % 2][r][:],
                                                            start=(k == 0), stop=(k == 2))
                                last.then_inc(gathered, 1)

                        def more_rounds(c, s):
                            hold(pe, top_ready, c + 1, pe_passed)
                            high = pe.value_load(top[s][0:1, 0:1], min_val=0, max_val=2 * P)
                            with pe.If(high >= 2 * ROUNDS + 1):
                                hold(pe, maxed, ROUNDS * NG * (c + 1), pe_passed)
                                with pe.Fori(2 * ROUNDS + 1, high + 1, 2):
                                    before = pe.snap(n_over)
                                    for g in range(NG):
                                        pe.wait_ge(o_pick, before + g + 1)
                                        if g >= 4:
                                            pe.wait_ge(o_maxed, before + g - 3)
                                        for k in range(3):
                                            last = nc.tensor.matmul(gath_ps[g % 4][:], hcur[s][:, k, :], opick[g][:],
                                                                    start=(k == 0), stop=(k == 2))
                                        last.then_inc(o_gathered, 1)
                                    pe.wait_ge(o_maxed, before + NG)
                                    pe.reg_add(n_over, n_over, NG)

                        def body(c, s, reuse, more):
                            for g in range(NG):
                                if more:
                                    front(c + 1, 1 - s, g, True)
                                gather(c, s, g, reuse)
                            more_rounds(c, s)

                        for g in range(NG):
                            front(0, 0, g, False)
                        body(0, 0, False, True)
                        body(1, 1, True, True)
                        with pe.Fori(1, NC // 2 - 1) as t:
                            for s in range(2):
                                body(chunk(t, s), s, True, True)
                        body(NC - 2, 0, True, True)
                        body(NC - 1, 1, True, False)

                    @block.gpsimd
                    def _(pool):
                        def picks(c, s, g, reuse):
                            u = NG * c + g
                            if reuse or g >= 2:
                                pool.wait_ge(gathered, ROUNDS * (u - 1))
                            hold(pool, code_ready, u + 1, pool_passed)
                            for r in range(ROUNDS):
                                nc.gpsimd.tensor_scalar(pick[g % 2][r][:], code[s][:, g * GW:(g + 1) * GW],
                                                        float(2 * r + 1), None, ALU.is_equal).then_inc(pick_ready, 1)
                            if g == 5:
                                hold(pool, rowmax_ready, c + 1, pool_passed)
                                nc.gpsimd.partition_all_reduce(allmax[:], rowmax[:], P, bass.bass_isa.ReduceOp.max
                                                               ).then_inc(allmax_ready, 1)
                        for s in range(2):
                            for g in range(NG):
                                picks(s, s, g, s == 1)
                        with pool.Fori(1, NC // 2) as t:
                            for s in range(2):
                                for g in range(NG):
                                    picks(chunk(t, s), s, g, True)

                    @block.vector
                    def _(vec):
                        n_over = vec.alloc_register("vec_over")
                        vec.reg_mov(n_over, 0)
                        n_want = vec.alloc_register("vec_want")
                        vec.reg_mov(n_want, 0)

                        def maxima(c, s, t, g):
                            u = NG * c + g
                            if g == 2:
                                vec.wait_ge(last_in[s], 16 * (t + 1))
                                nc.vector.tensor_reduce(rowmax[:], last_row[s][:], AX.X, ALU.max).then_inc(rowmax_ready, 1)
                            if g == 7:
                                vec.wait_ge(allmax_ready, c + 1)
                                nc.vector.tensor_copy(top[s][:], allmax[0:1, :]).then_inc(top_ready, 1)
                            for r in range(ROUNDS):
                                vec.wait_ge(gathered, ROUNDS * u + r + 1)
                                view = acc[:, g * GW:(g + 1) * GW]
                                nc.vector.tensor_tensor(view, gath_ps[r][:], view, ALU.max).then_inc(maxed, 1)
                                vec.wait_ge(maxed, ROUNDS * u + r + 1)

                        def more_rounds(c, s):
                            hold(vec, top_ready, c + 1, vec_passed)
                            high = vec.value_load(top[s][0:1, 0:1], min_val=0, max_val=2 * P)
                            with vec.If(high >= 2 * ROUNDS + 1):
                                vec.reg_add(n_want, n_want, 1)
                                nc.vector.memset(want[:], float(2 * ROUNDS + 1)).then_inc(want_set, 1)
                                with vec.Fori(2 * ROUNDS + 1, high + 1, 2):
                                    before = vec.snap(n_over)
                                    turn = vec.snap(n_want)
                                    vec.wait_ge(want_set, turn)
                                    for g in range(NG):
                                        nc.vector.tensor_scalar(opick[g][:], code[s][:, g * GW:(g + 1) * GW],
                                                                want[:, 0:1], None, ALU.is_equal).then_inc(o_pick, 1)
                                    for g in range(NG):
                                        vec.wait_ge(o_gathered, before + g + 1)
                                        view = acc[:, g * GW:(g + 1) * GW]
                                        nc.vector.tensor_tensor(view, gath_ps[g % 4][:], view, ALU.max).then_inc(o_maxed, 1)
                                    vec.wait_ge(o_maxed, before + NG)
                                    vec.reg_add(n_over, n_over, NG)
                                    nc.vector.tensor_scalar(want[:], want[:], 2.0, None, ALU.add).then_inc(want_set, 1)
                                    vec.reg_add(n_want, n_want, 1)
                                turn = vec.snap(n_want)
                                hold(vec, want_set, turn, vec_passed)

                        def body(c, s, t):
                            for g in range(NG):
                                maxima(c, s, t, g)
                            more_rounds(c, s)
                            vec.sem_inc(chunk_done, 1)

                        with vec.Fori(0, NC // 2) as t:
                            for s in range(2):
                                body(chunk(t, s), s, t)

        second = ExitStack()
        with second:
            wh = sb("wh", [P, NC, E], F32, second)
            h2t = acc
            scope = ExitStack()
            with scope:
                h2 = sb("h2", [P, NC, F], F32, scope)
                x1_ps, x1_done, h2_ready, h2t_ps, h2t_done = (sem("x1_ps"), sem("x1_done"), sem("h2_ready"),
                                                              sem("h2t_ps"), sem("h2t_done"))
                vec2, var2_ready, sqrt2_done, wh_ps, wh_done = (sem("vec2"), sem("var2_ready"), sem("sqrt2_done"),
                                                                sem("wh_ps"), sem("wh_done"))
                NW = NC // 2
                with nc.Block() as block:
                    @block.tensor
                    def _(pe):
                        for g in range(NG):
                            if g >= 4:
                                pe.wait_ge(x1_done, g - 3)
                            for k in range(GB):
                                b = GB * g + k
                                last = nc.tensor.transpose(banks[g % 4][:, k * P:(k + 1) * P], acc[:, b * P:(b + 1) * P],
                                                           ident[:])
                            last.then_inc(x1_ps, 1)
                        pe.wait_ge(h2_ready, 1)
                        for g in range(NG):
                            if g >= 4:
                                pe.wait_ge(h2t_done, g - 3)
                            for k in range(GB):
                                last = nc.tensor.transpose(banks[4 + g % 4][:, k * P:(k + 1) * P],
                                                           h2[:, GB * g + k, :], ident[:])
                            last.then_inc(h2t_ps, 1)
                        for w in range(NW):
                            pe.wait_ge(h2t_done, (2 * w) // GB + 1)
                            if w >= 4:
                                pe.wait_ge(wh_done, w - 3)
                            for k in range(2):
                                c = 2 * w + k
                                last = nc.tensor.matmul(banks[w % 4][:, k * E:(k + 1) * E], h2t[:, c * P:(c + 1) * P],
                                                        w_ext[:], start=True, stop=True)
                            last.then_inc(wh_ps, 1)

                    @block.vector
                    def _(vec):
                        link = linker(vec, vec2)
                        for g in range(NG):
                            vec.wait_ge(x1_ps, g + 1)
                            view = xs[:, GB * g:GB * (g + 1), :]
                            nc.vector.tensor_tensor(view, banks[g % 4][:].rearrange("p (b f) -> p b f", f=F), view,
                                                    ALU.add).then_inc(x1_done, 1)
                        vec.wait_ge(x1_done, NG)
                        layernorm_relu(vec, link, h2, var2_ready, sqrt2_done, 1)
                        vec.sem_inc(h2_ready, 1)

                    @block.scalar
                    def _(act):
                        act.wait_ge(var2_ready, 1)
                        nc.scalar.activation(rstd[:], rstd[:], ACT.Sqrt).then_inc(sqrt2_done, 1)
                        for g in range(NG):
                            act.wait_ge(h2t_ps, g + 1)
                            nc.scalar.copy(h2t[:, g * GW:(g + 1) * GW], banks[4 + g % 4][:]).then_inc(h2t_done, 1)
                        for w in range(NW):
                            act.wait_ge(wh_ps, w + 1)
                            nc.scalar.copy(wh[:, 2 * w:2 * w + 2, :],
                                           banks[w % 4][:, 0:2 * E].rearrange("p (k e) -> p k e", e=E)).then_inc(wh_done, 1)
                        act.wait_ge(wh_done, NW)

            general_attention(nc, sem, sb, banks, locals())


def general_attention(nc, sem, sb, banks, v):
    N, F, H, D, NC, NG, GW, GB, E = (v[k] for k in ("N", "F", "H", "D", "NC", "NG", "GW", "GB", "E"))
    wh, h2t, xs, ident, w_ext = v["wh"], v["h2t"], v["xs"], v["ident"], v["w_ext"]
    adj_rows, out_rows = v["adj_rows"], v["out_rows"]
    scope = ExitStack()
    with scope:
        wrep = sb("wrep", [P, H, P], F32, scope)
        drow = sb("drow", [P, H, N], F32, scope)
        arow = sb("arow", [P, N], I32, scope)
        keep = sb("keep", [P, N], F32, scope)
        fill = sb("fill", [P, N], F32, scope)
        e = sb("e", [P, N], F32, scope)
        pt = arow[:].bitcast(F32)
        ssrc = sb("ssrc", [P, H], F32, scope)
        nmax = sb("nmax", [P, 1], F32, scope)
        den = sb("den", [P, H], F32, scope)
        rden = sb("rden", [P, 1], F32, scope)
        o = sb("o", [P, F], F32, scope)
        neg = sb("neg", [P, F], F32, scope)
        wrep_ready, drow_ps, drow_done = sem("wrep_ready"), sem("drow_ps"), sem("drow_done")
        arow_in, arow_free, e_ready, p_ready, p_ps, p_evac, pv, vec3, s_elu, elu_exp, o_ready, stored = (
            sem(n) for n in ("arow_in", "arow_free", "e_ready", "p_ready", "p_ps", "p_evac", "pv", "vec3", "s_elu",
                             "elu_exp", "o_ready", "stored"))
        VL = 3 + 6 * H + 3
        with nc.Block() as block:
            @block.sync
            def _(sp):
                with sp.Fori(0, NC) as b:
                    sp.wait_ge(arow_free, b + 1)
                    sp.dma_start(arow[:], adj_rows[b]).then_inc(arow_in, 16)
                    sp.wait_ge(o_ready, b + 1)
                    sp.dma_start(out_rows[b], o[:]).then_inc(stored, 16)
                sp.wait_ge(stored, 16 * NC)

            @block.tensor
            def _(pe):
                pe.wait_ge(wrep_ready, 1)
                for h in range(H):
                    for g in range(NG):
                        n = NG * h + g
                        if n >= 4:
                            pe.wait_ge(drow_done, n - 3)
                        nc.tensor.matmul(banks[n % 4][:], wrep[:, h, :], h2t[:, g * GW:(g + 1) * GW],
                                         start=True, stop=True).then_inc(drow_ps, 1)
                pe.wait_ge(drow_done, NG * H)
                with pe.Fori(0, NC) as b:
                    for h in range(H):
                        i = b * H + h
                        pe.wait_ge(p_ready, i + 1)
                        for g in range(NG):
                            if g >= 2:
                                pe.wait_ge(p_evac, NG * i + g - 1)
                            for k in range(GB):
                                c = GB * g + k
                                last = nc.tensor.transpose(banks[g % 2][:, k * P:(k + 1) * P], e[:, c * P:(c + 1) * P],
                                                           ident[:])
                            last.then_inc(p_ps, 1)
                        pe.wait_ge(p_evac, NG * (i + 1))
                        for c in range(NC):
                            last = nc.tensor.matmul(banks[2 + h][:, 0:D], pt[:, c * P:(c + 1) * P],
                                                    wh[:, c, h * D:(h + 1) * D], start=(c == 0), stop=(c == NC - 1))
                        last.then_inc(pv, 1)

            @block.scalar
            def _(act):
                for n in range(NG * H):
                    act.wait_ge(drow_ps, n + 1)
                    nc.scalar.copy(drow[:, n // NG, (n % NG) * GW:(n % NG + 1) * GW], banks[n % 4][:]).then_inc(drow_done, 1)
                with act.Fori(0, NC) as b:
                    for h in range(H):
                        i = b * H + h
                        act.wait_ge(e_ready, i + 1)
                        nc.scalar.activation(e[:], e[:], ACT.Exp, bias=nmax[:, 0:1], scale=1.0,
                                             accum_out=den[:, h:h + 1]).then_inc(p_ready, 1)
                        for g in range(NG):
                            act.wait_ge(p_ps, NG * i + g + 1)
                            if h > 0 and g == 0:
                                act.wait_ge(pv, i)
                            nc.scalar.copy(pt[:, g * GW:(g + 1) * GW], banks[g % 2][:]).then_inc(p_evac, 1)
                    act.wait_ge(s_elu, b + 1)
                    nc.scalar.activation(neg[:], neg[:], ACT.Exp).then_inc(elu_exp, 1)

            @block.vector
            def _(vec):
                nc.vector.tensor_copy(wrep[:], w_ext[:, F + H:E].unsqueeze(2).to_broadcast([P, H, P])).then_inc(wrep_ready, 1)
                vec.wait_ge(drow_done, NG * H)
                vec.sem_inc(arow_free, 1)
                with vec.Fori(0, NC) as b:
                    count = [0]

                    def link(ins):
                        count[0] += 1
                        ins.then_inc(vec3, 1)
                        vec.wait_ge(vec3, VL * b + count[0])
                    vec.wait_ge(arow_in, 16 * (b + 1))
                    link(nc.vector.tensor_scalar(keep[:], arow[:], 0.0, None, ALU.is_gt))
                    link(nc.vector.tensor_scalar(fill[:], keep[:], 1.0, NEG_INF, ALU.subtract, ALU.mult))
                    link(nc.vector.tensor_copy(ssrc[:], wh[:, bass.ds(b, 1), F:F + H].rearrange("p o e -> p (o e)")))
                    for h in range(H):
                        i = b * H + h
                        if h > 0:
                            vec.wait_ge(p_evac, NG * i)
                        link(nc.vector.tensor_scalar(e[:], drow[:, h, :], ssrc[:, h:h + 1], None, ALU.add))
                        link(nc.vector.scalar_tensor_tensor(e[:], e[:], ALPHA, e[:], ALU.mult, ALU.max))
                        link(nc.vector.tensor_tensor(e[:], e[:], keep[:], ALU.mult))
                        link(nc.vector.tensor_tensor(e[:], e[:], fill[:], ALU.add))
                        link(nc.vector.tensor_reduce(nmax[:], e[:], AX.X, ALU.max, negate=True))
                        vec.sem_inc(e_ready, 1)
                        vec.wait_ge(p_ready, i + 1)
                        link(nc.vector.reciprocal(rden[:], den[:, h:h + 1]))
                        vec.wait_ge(pv, i + 1)
                        ins = nc.vector.tensor_scalar(o[:, h * D:(h + 1) * D], banks[2 + h][:, 0:D], rden[:, 0:1], None,
                                                      ALU.mult)
                    ins.then_inc(arow_free, 1)
                    vec.wait_ge(arow_free, b + 2)
                    nc.vector.tensor_scalar(neg[:], o[:], 0.0, None, ALU.min).then_inc(s_elu, 1)
                    vec.wait_ge(elu_exp, b + 1)
                    link(nc.vector.tensor_scalar(o[:], o[:], 0.0, None, ALU.max))
                    link(nc.vector.scalar_tensor_tensor(o[:], neg[:], -1.0, o[:], ALU.add, ALU.add))
                    link(nc.vector.tensor_tensor(o[:], o[:], xs[:, bass.ds(b, 1), :].rearrange("p o f -> p (o f)"), ALU.add))
                    vec.sem_inc(o_ready, 1)
                    vec.wait_ge(stored, 16 * (b + 1))


_INS = ["x", "adj", "L1_gnn_W", "L1_gnn_a"]


def kernel(**inputs):
    import numpy as _np
    import concourse.bacc as _bacc
    from concourse import mybir as _mybir
    from concourse.bass_utils import run_bass_kernel_spmd as _run

    nc = _bacc.Bacc("TRN2", target_bir_lowering=False, num_devices=1)
    arrays, args = {}, []
    for name in _INS:
        a = _np.ascontiguousarray(inputs[name])
        arrays[f"in_{name}"] = a
        args.append(nc.dram_tensor(f"in_{name}", a.shape, _mybir.dt.from_np(a.dtype), kind="ExternalInput").ap())
    out = nc.dram_tensor("out_x", inputs["x"].shape, _mybir.dt.float32, kind="ExternalOutput").ap()
    emit(nc, *args, out)
    r = _run(nc, [arrays], core_ids=[0])
    return r.results[0]["out_x"]
```

```python
import numpy as np
import concourse.bass as bass
from concourse import mybir
from contextlib import ExitStack

F32 = mybir.dt.float32
BF16 = mybir.dt.bfloat16
I32 = mybir.dt.int32
ALU = mybir.AluOpType
ACT = mybir.ActivationFunctionType
AX = mybir.AxisListType

P = 128
ROUNDS = 4
EPS = 1e-5
ALPHA = 0.2
NEG_INF = 9000000000000000.0
SPREAD = 60.0
LARGEST = 1e6


def hold(engine, semaphore, value, passed):
    engine.wait_ge(semaphore, value)
    engine.sem_inc(passed, 1)


def emit(nc, x_dram, adj_dram, w_dram, a_dram, out_dram):
    N, F = x_dram.shape
    H, D2 = a_dram.shape[1], a_dram.shape[2]
    D = D2 // 2
    NC = N // P
    GW = 512
    NG = N // GW
    GB = GW // P
    E = F + 2 * H
    adj_chunks = adj_dram.rearrange("(b p) (c j) -> c p b j", p=P, j=P)
    adj_rows = adj_dram.rearrange("(b p) j -> b p j", p=P)
    x_view = x_dram.rearrange("(b p) f -> p b f", p=P)
    mask_dram = nc.dram_tensor("mask_t_dram", (N, N), BF16, kind="Internal").ap()
    mask_rows = mask_dram.rearrange("(c p) i -> c p i", p=P)
    out_rows = out_dram.rearrange("(b p) f -> b p f", p=P)

    ctx = ExitStack()

    def sem(name):
        return ctx.enter_context(nc.semaphore(name))

    with ctx:
        def sb(name, shape, dt, where=ctx):
            return where.enter_context(nc.sbuf_tensor(name, shape, dt))

        banks = [ctx.enter_context(nc.psum_tensor(f"bank{i}", [P, 512], F32)) for i in range(8)]

        ident = sb("ident", [P, P], F32)
        xs = sb("xs", [P, NC, F], F32)
        w_ext = sb("w_ext", [P, E], F32)
        acc = sb("acc", [P, N], F32)
        stats = sb("stats", [P, NC, 6], F32)
        mv = sb("mv", [P, NC, 2], F32)
        rstd = sb("rstd", [P, NC], F32)
        epst = sb("epst", [P, 1], F32)

        def layernorm_relu(vec, link, h, sqrt_in_ready, sqrt_done, count):
            for b in range(NC):
                last = nc.vector.bn_stats(stats[:, b, :], xs[:, b, :])
            link(last)
            for b in range(NC):
                last = nc.vector.bn_aggr(mv[:, b, :], stats[:, b, :])
            link(last)
            nc.vector.tensor_scalar(rstd[:], mv[:, :, 1], EPS, None, ALU.add).then_inc(sqrt_in_ready, 1)
            link(nc.vector.tensor_tensor(h[:], xs[:], mv[:, :, 0:1].to_broadcast([P, NC, F]), ALU.subtract))
            vec.wait_ge(sqrt_done, count)
            link(nc.vector.reciprocal(rstd[:], rstd[:]))
            link(nc.vector.tensor_tensor(h[:], h[:], rstd[:].unsqueeze(2).to_broadcast([P, NC, F]), ALU.mult))
            link(nc.vector.tensor_scalar(h[:], h[:], 0.0, None, ALU.max))

        def linker(vec, s):
            count = [0]

            def link(ins):
                count[0] += 1
                ins.then_inc(s, 1)
                vec.wait_ge(s, count[0])
            return link

        first = ExitStack()
        with first:
            ident16 = sb("ident16", [P, P], BF16, first)
            rank_w = sb("rank_w", [P, P], BF16, first)
            hparts = sb("hparts", [P, NC, 3, F], BF16, first)
            adjs = [sb(f"adjs{i}", [P, NC, P], I32, first) for i in range(2)]
            adj_in = [sem(f"adj_in{i}") for i in range(2)]

            scope = ExitStack()
            with scope:
                h = sb("h", [P, NC, F], F32, scope)
                wt = sb("wt", [P, P], F32, scope)
                a_diag = sb("a_diag", [P, 2 * H], F32, scope)
                x_in, w_in, a_in = sem("x_in"), sem("w_in"), sem("a_in")
                vec0, a_zero, ident_built, rank_built = sem("vec0"), sem("a_zero"), sem("ident_built"), sem("rank_built")
                pool0 = sem("pool0")
                var_ready, sqrt_done = sem("var_ready"), sem("sqrt_done")
                wt_ps, wt_sb, wa_ps, wa_sb = sem("wt_ps"), sem("wt_sb"), sem("wa_ps"), sem("wa_sb")

                with nc.Block() as block:
                    @block.sync
                    def _(sp):
                        sp.dma_start(xs[:], x_view).then_inc(x_in, 16)
                        sp.dma_start(w_ext[:, 0:F], w_dram).then_inc(w_in, 16)
                        for s in range(2):
                            sp.dma_start(adjs[s][:], adj_chunks[s]).then_inc(adj_in[s], 16)
                        sp.wait_ge(a_zero, 1)
                        for k in range(2):
                            for hd in range(H):
                                sp.dma_start(a_diag[hd * D:(hd + 1) * D, k * H + hd:k * H + hd + 1],
                                             a_dram[0, hd, k * D:(k + 1) * D].unsqueeze(1)).then_inc(a_in, 16)

                    @block.gpsimd
                    def _(pool):
                        nc.gpsimd.memset(a_diag[:], 0.0).then_inc(a_zero, 1)
                        nc.gpsimd.memset(ident[:], 0.0).then_inc(pool0, 1)
                        nc.gpsimd.memset(rank_w[:], 2.0).then_inc(pool0, 1)
                        pool.wait_ge(pool0, 2)
                        nc.gpsimd.affine_select(out=ident[:], in_=ident[:], compare_op=ALU.not_equal, fill=1.0,
                                                base=0, pattern=[[-1, P]], channel_multiplier=1).then_inc(pool0, 1)
                        nc.gpsimd.affine_select(out=rank_w[:], in_=rank_w[:], compare_op=ALU.is_gt, fill=0.0,
                                                base=0, pattern=[[1, P]], channel_multiplier=-1).then_inc(pool0, 1)
                        pool.wait_ge(pool0, 4)
                        nc.gpsimd.tensor_copy(ident16[:], ident[:]).then_inc(ident_built, 1)
                        pool.wait_ge(ident_built, 1)
                        nc.gpsimd.tensor_tensor(rank_w[:], rank_w[:], ident16[:], ALU.add).then_inc(rank_built, 1)
                        pool.wait_ge(rank_built, 1)

                    @block.scalar
                    def _(act):
                        act.wait_ge(wt_ps, 1)
                        nc.scalar.copy(wt[:], banks[0][:, 0:P]).then_inc(wt_sb, 1)
                        act.wait_ge(wa_ps, 1)
                        nc.scalar.copy(w_ext[:, F:E], banks[1][:, 0:2 * H]).then_inc(wa_sb, 1)
                        act.wait_ge(var_ready, 1)
                        nc.scalar.activation(rstd[:], rstd[:], ACT.Sqrt).then_inc(sqrt_done, 1)
                        act.wait_ge(wa_sb, 1)

                    @block.tensor
                    def _(pe):
                        pe.wait_ge(ident_built, 1)
                        pe.wait_ge(w_in, 16)
                        nc.tensor.transpose(banks[0][:, 0:P], w_ext[:, 0:F], ident[:]).then_inc(wt_ps, 1)
                        pe.wait_ge(wt_sb, 1)
                        pe.wait_ge(a_in, 16 * 2 * H)
                        nc.tensor.matmul(banks[1][:, 0:2 * H], wt[:], a_diag[:], start=True, stop=True).then_inc(wa_ps, 1)

                    @block.vector
                    def _(vec):
                        link = linker(vec, vec0)
                        link(nc.vector.memset(acc[:], 0.0))
                        vec.wait_ge(x_in, 16)
                        layernorm_relu(vec, link, h, var_ready, sqrt_done, 1)
                        for k in range(2):
                            link(nc.vector.tensor_copy(hparts[:, :, k, :], h[:]))
                            if k == 0:
                                link(nc.vector.tensor_tensor(h[:], h[:], hparts[:, :, k, :], ALU.subtract))
                        link(nc.vector.tensor_tensor(hparts[:, :, 2, :], h[:], hparts[:, :, 1, :], ALU.subtract))

            scope = ExitStack()
            with scope:
                adj16 = [sb(f"adj16_{i}", [P, GW], BF16, scope) for i in range(2)]
                mask_t = [sb(f"mask_t{i}", [P, N], BF16, scope) for i in range(2)]
                code = [sb(f"code{i}", [P, N], BF16, scope) for i in range(2)]
                hcur = [sb(f"hcur{i}", [P, 3, F], BF16, scope) for i in range(2)]
                pick = [[sb(f"pick{i}_{r}", [P, GW], BF16, scope) for r in range(ROUNDS)] for i in range(2)]
                opick = [sb(f"opick{g}", [P, GW], BF16, scope) for g in range(NG)]
                last_row = [sb(f"last_row{i}", [P, N // P], BF16, scope) for i in range(2)]
                rowmax = sb("rowmax", [P, 1], F32, scope)
                allmax = sb("allmax", [P, 1], F32, scope)
                top = [sb(f"top{i}", [1, 1], I32, scope) for i in range(2)]
                want = sb("want", [P, 1], F32, scope)

                adj16_ready = sem("adj16_ready")
                turned = sem("turned")
                mask_ready = sem("mask_ready")
                coded = sem("coded")
                code_ready = sem("code_ready")
                hcur_ready = sem("hcur_ready")
                pick_ready = sem("pick_ready")
                gathered = sem("gathered")
                mask_out = [sem(f"mask_out{i}") for i in range(2)]
                pool_passed, pe_passed, vec_passed = sem("pool_passed"), sem("pe_passed"), sem("vec_passed")
                maxed = sem("maxed")
                chunk_done = sem("chunk_done")
                last_in = [sem(f"last_in{i}") for i in range(2)]
                rowmax_ready, allmax_ready, top_ready = sem("rowmax_ready"), sem("allmax_ready"), sem("top_ready")
                o_pick, o_gathered, o_maxed, want_set = sem("o_pick"), sem("o_gathered"), sem("o_maxed"), sem("want_set")

                turn_ps = [banks[i][:, 0:GW // 2].bitcast(BF16) for i in range(2)]
                code_ps = [banks[2 + i] for i in range(2)]
                gath_ps = [banks[4 + r] for r in range(ROUNDS)]
                chunk = lambda t, s: 2 * t + s

                with nc.Block() as block:
                    @block.sync
                    def _(sp):
                        def serve(c, s, t, load):
                            if load:
                                sp.wait_ge(adj16_ready, NG * (c + 1))
                                sp.dma_start(adjs[s][:], adj_chunks[c + 2]).then_inc(adj_in[s], 16)
                            sp.wait_ge(mask_ready, NG * (c + 1))
                            sp.dma_start(mask_rows[c], mask_t[s][:]).then_inc(mask_out[s], 16)
                            sp.wait_ge(code_ready, NG * (c + 1))
                            sp.dma_start(last_row[s][:], code[s][P - 1:P, :]
                                         ).then_inc(last_in[s], 16)
                        with sp.Fori(0, NC // 2 - 1) as t:
                            for s in range(2):
                                serve(chunk(t, s), s, t, True)
                        for s in range(2):
                            serve(NC - 2 + s, s, NC // 2 - 1, False)
                        for s in range(2):
                            sp.wait_ge(mask_out[s], 16 * (NC // 2))

                    @block.scalar
                    def _(act):
                        def front(c, s, t, g, reuse):
                            u = NG * c + g
                            b = g % 2
                            if g == 0:
                                act.wait_ge(adj_in[s], 16 * (t + 1))
                            if reuse or g >= 2:
                                act.wait_ge(turned, u - 1)
                            nc.scalar.copy(adj16[b][:], adjs[s][:, GB * g:GB * (g + 1), :]).then_inc(adj16_ready, 1)
                            act.wait_ge(turned, u + 1)
                            if reuse and g == 0:
                                act.wait_ge(mask_out[s], 16 * t)
                            nc.scalar.copy(mask_t[s][:, g * GW:(g + 1) * GW], turn_ps[b]).then_inc(mask_ready, 1)
                            act.wait_ge(coded, u + 1)
                            if reuse and g == 0:
                                act.wait_ge(chunk_done, c - 1)
                            nc.scalar.copy(code[s][:, g * GW:(g + 1) * GW], code_ps[b][:]).then_inc(code_ready, 1)
                            if g == 0:
                                nc.scalar.copy(hcur[s][:], hparts[:, bass.ts(c, 1), :, :] if not isinstance(c, int)
                                               else hparts[:, c:c + 1, :, :]).then_inc(hcur_ready, 1)

                        for s in range(2):
                            for g in range(NG):
                                front(s, s, 0, g, False)
                        with act.Fori(1, NC // 2) as t:
                            for s in range(2):
                                for g in range(NG):
                                    front(chunk(t, s), s, t, g, True)

                    @block.tensor
                    def _(pe):
                        n_over = pe.alloc_register("pe_over")
                        pe.reg_mov(n_over, 0)

                        def front(c, s, g, reuse):
                            u = NG * c + g
                            b = g % 2
                            pe.wait_ge(adj16_ready, u + 1)
                            if reuse or g >= 2:
                                pe.wait_ge(mask_ready, u - 1)
                            for k in range(GB):
                                last = nc.tensor.transpose(turn_ps[b][:, k * P:(k + 1) * P],
                                                           adj16[b][:, k * P:(k + 1) * P], ident16[:])
                            last.then_inc(turned, 1)
                            pe.wait_ge(mask_ready, u + 1)
                            if reuse or g >= 2:
                                pe.wait_ge(code_ready, u - 1)
                            nc.tensor.matmul(code_ps[b][:], rank_w[:], mask_t[s][:, g * GW:(g + 1) * GW],
                                             start=True, stop=True).then_inc(coded, 1)

                        def gather(c, s, g, reuse):
                            u = NG * c + g
                            if g == 0:
                                pe.wait_ge(hcur_ready, c + 1)
                            for r in range(ROUNDS):
                                pe.wait_ge(pick_ready, ROUNDS * u + r + 1)
                                if reuse or g >= 1:
                                    pe.wait_ge(maxed, ROUNDS * (u - 1) + r + 1)
                                for k in range(3):
                                    last = nc.tensor.matmul(gath_ps[r][:], hcur[s][:, k, :], pick[g % 2][r][:],
                                                            start=(k == 0), stop=(k == 2))
                                last.then_inc(gathered, 1)

                        def more_rounds(c, s):
                            hold(pe, top_ready, c + 1, pe_passed)
                            high = pe.value_load(top[s][0:1, 0:1], min_val=0, max_val=2 * P)
                            with pe.If(high >= 2 * ROUNDS + 1):
                                hold(pe, maxed, ROUNDS * NG * (c + 1), pe_passed)
                                with pe.Fori(2 * ROUNDS + 1, high + 1, 2):
                                    before = pe.snap(n_over)
                                    for g in range(NG):
                                        pe.wait_ge(o_pick, before + g + 1)
                                        if g >= 4:
                                            pe.wait_ge(o_maxed, before + g - 3)
                                        for k in range(3):
                                            last = nc.tensor.matmul(gath_ps[g % 4][:], hcur[s][:, k, :], opick[g][:],
                                                                    start=(k == 0), stop=(k == 2))
                                        last.then_inc(o_gathered, 1)
                                    pe.wait_ge(o_maxed, before + NG)
                                    pe.reg_add(n_over, n_over, NG)

                        def body(c, s, reuse, more):
                            for g in range(NG):
                                if more:
                                    front(c + 1, 1 - s, g, True)
                                gather(c, s, g, reuse)
                            more_rounds(c, s)

                        for g in range(NG):
                            front(0, 0, g, False)
                        body(0, 0, False, True)
                        body(1, 1, True, True)
                        with pe.Fori(1, NC // 2 - 1) as t:
                            for s in range(2):
                                body(chunk(t, s), s, True, True)
                        body(NC - 2, 0, True, True)
                        body(NC - 1, 1, True, False)

                    @block.gpsimd
                    def _(pool):
                        with pool.Fori(0, NC) as c:
                            hold(pool, rowmax_ready, c + 1, pool_passed)
                            nc.gpsimd.partition_all_reduce(allmax[:], rowmax[:], P, bass.bass_isa.ReduceOp.max
                                                           ).then_inc(allmax_ready, 1)

                    @block.vector
                    def _(vec):
                        n_over = vec.alloc_register("vec_over")
                        vec.reg_mov(n_over, 0)
                        n_want = vec.alloc_register("vec_want")
                        vec.reg_mov(n_want, 0)

                        def pick_one(c, s, g, r):
                            if r == 0:
                                vec.wait_ge(code_ready, NG * c + g + 1)
                            nc.vector.tensor_scalar(pick[g % 2][r][:], code[s][:, g * GW:(g + 1) * GW],
                                                    float(2 * r + 1), None, ALU.is_equal).then_inc(pick_ready, 1)

                        def maxima(c, s, t, g, nxt):
                            u = NG * c + g
                            if g == 2:
                                vec.wait_ge(last_in[s], 16 * (t + 1))
                                nc.vector.tensor_reduce(rowmax[:], last_row[s][:], AX.X, ALU.max).then_inc(rowmax_ready, 1)
                            if g == 7:
                                vec.wait_ge(allmax_ready, c + 1)
                                nc.vector.tensor_copy(top[s][:], allmax[0:1, :]).then_inc(top_ready, 1)
                            for r in range(ROUNDS):
                                if nxt is not None:
                                    pick_one(*nxt, r)
                                if r >= 1:
                                    vec.wait_ge(maxed, ROUNDS * u + r)
                                vec.wait_ge(gathered, ROUNDS * u + r + 1)
                                view = acc[:, g * GW:(g + 1) * GW]
                                nc.vector.tensor_tensor(view, gath_ps[r][:], view, ALU.max).then_inc(maxed, 1)

                        def more_rounds(c, s):
                            vec.wait_ge(maxed, ROUNDS * NG * (c + 1))
                            hold(vec, top_ready, c + 1, vec_passed)
                            high = vec.value_load(top[s][0:1, 0:1], min_val=0, max_val=2 * P)
                            with vec.If(high >= 2 * ROUNDS + 1):
                                vec.reg_add(n_want, n_want, 1)
                                nc.vector.memset(want[:], float(2 * ROUNDS + 1)).then_inc(want_set, 1)
                                with vec.Fori(2 * ROUNDS + 1, high + 1, 2):
                                    before = vec.snap(n_over)
                                    turn = vec.snap(n_want)
                                    vec.wait_ge(want_set, turn)
                                    for g in range(NG):
                                        nc.vector.tensor_scalar(opick[g][:], code[s][:, g * GW:(g + 1) * GW],
                                                                want[:, 0:1], None, ALU.is_equal).then_inc(o_pick, 1)
                                    for g in range(NG):
                                        vec.wait_ge(o_gathered, before + g + 1)
                                        view = acc[:, g * GW:(g + 1) * GW]
                                        nc.vector.tensor_tensor(view, gath_ps[g % 4][:], view, ALU.max).then_inc(o_maxed, 1)
                                    vec.wait_ge(o_maxed, before + NG)
                                    vec.reg_add(n_over, n_over, NG)
                                    nc.vector.tensor_scalar(want[:], want[:], 2.0, None, ALU.add).then_inc(want_set, 1)
                                    vec.reg_add(n_want, n_want, 1)
                                turn = vec.snap(n_want)
                                hold(vec, want_set, turn, vec_passed)

                        def body(c, s, t, more=True):
                            for g in range(NG):
                                nxt = (c, s, g + 1) if g < NG - 1 else (c + 1, 1 - s, 0) if more else None
                                maxima(c, s, t, g, nxt)
                            more_rounds(c, s)
                            vec.sem_inc(chunk_done, 1)

                        for r in range(ROUNDS):
                            pick_one(0, 0, 0, r)
                        with vec.Fori(0, NC // 2 - 1) as t:
                            for s in range(2):
                                body(chunk(t, s), s, t)
                        body(NC - 2, 0, NC // 2 - 1)
                        body(NC - 1, 1, NC // 2 - 1, False)

        second = ExitStack()
        with second:
            wh = sb("wh", [P, NC, E], F32, second)
            h2t = acc
            scope = ExitStack()
            with scope:
                h2 = sb("h2", [P, NC, F], F32, scope)
                x1_ps, x1_done, h2_ready, h2t_ps, h2t_done = (sem("x1_ps"), sem("x1_done"), sem("h2_ready"),
                                                              sem("h2t_ps"), sem("h2t_done"))
                vec2, var2_ready, sqrt2_done, wh_ps, wh_done = (sem("vec2"), sem("var2_ready"), sem("sqrt2_done"),
                                                                sem("wh_ps"), sem("wh_done"))
                NW = NC // 2
                with nc.Block() as block:
                    @block.tensor
                    def _(pe):
                        for g in range(NG):
                            if g >= 4:
                                pe.wait_ge(x1_done, g - 3)
                            for k in range(GB):
                                b = GB * g + k
                                last = nc.tensor.transpose(banks[g % 4][:, k * P:(k + 1) * P], acc[:, b * P:(b + 1) * P],
                                                           ident[:])
                            last.then_inc(x1_ps, 1)
                        pe.wait_ge(h2_ready, 1)
                        for g in range(NG):
                            if g >= 4:
                                pe.wait_ge(h2t_done, g - 3)
                            for k in range(GB):
                                last = nc.tensor.transpose(banks[4 + g % 4][:, k * P:(k + 1) * P],
                                                           h2[:, GB * g + k, :], ident[:])
                            last.then_inc(h2t_ps, 1)
                        for w in range(NW):
                            pe.wait_ge(h2t_done, (2 * w) // GB + 1)
                            if w >= 4:
                                pe.wait_ge(wh_done, w - 3)
                            for k in range(2):
                                c = 2 * w + k
                                last = nc.tensor.matmul(banks[w % 4][:, k * E:(k + 1) * E], h2t[:, c * P:(c + 1) * P],
                                                        w_ext[:], start=True, stop=True)
                            last.then_inc(wh_ps, 1)

                    @block.vector
                    def _(vec):
                        link = linker(vec, vec2)
                        for g in range(NG):
                            vec.wait_ge(x1_ps, g + 1)
                            view = xs[:, GB * g:GB * (g + 1), :]
                            nc.vector.tensor_tensor(view, banks[g % 4][:].rearrange("p (b f) -> p b f", f=F), view,
                                                    ALU.add).then_inc(x1_done, 1)
                        vec.wait_ge(x1_done, NG)
                        layernorm_relu(vec, link, h2, var2_ready, sqrt2_done, 1)
                        vec.sem_inc(h2_ready, 1)

                    @block.scalar
                    def _(act):
                        act.wait_ge(var2_ready, 1)
                        nc.scalar.activation(rstd[:], rstd[:], ACT.Sqrt).then_inc(sqrt2_done, 1)
                        for g in range(NG):
                            act.wait_ge(h2t_ps, g + 1)
                            nc.scalar.copy(h2t[:, g * GW:(g + 1) * GW], banks[4 + g % 4][:]).then_inc(h2t_done, 1)
                        for w in range(NW):
                            act.wait_ge(wh_ps, w + 1)
                            nc.scalar.copy(wh[:, 2 * w:2 * w + 2, :],
                                           banks[w % 4][:, 0:2 * E].rearrange("p (k e) -> p k e", e=E)).then_inc(wh_done, 1)
                        act.wait_ge(wh_done, NW)

            gmax = sb("gmax", [P, 2 * H], F32, second)
            flag = sb("flag", [P, 1], I32, second)
            scope = ExitStack()
            with scope:
                lmax = sb("lmax", [P, 2 * H], F32, scope)
                test = sb("test", [P, 3], F32, scope)
                spread = sb("spread", [P, H], F32, scope)
                vec4, lmax_ready, gmax_ready = sem("vec4"), sem("lmax_ready"), sem("gmax_ready")
                with nc.Block() as block:
                    @block.gpsimd
                    def _(pool):
                        pool.wait_ge(lmax_ready, 1)
                        nc.gpsimd.partition_all_reduce(gmax[:], lmax[:], P, bass.bass_isa.ReduceOp.max).then_inc(gmax_ready, 1)

                    @block.vector
                    def _(vec):
                        link = linker(vec, vec4)
                        dst = wh[:, :, F + H:E].rearrange("p c h -> p h c")
                        link(nc.vector.tensor_reduce(lmax[:, 0:H], dst, AX.X, ALU.max))
                        link(nc.vector.tensor_reduce(lmax[:, H:2 * H], dst, AX.X, ALU.min, negate=True))
                        vec.sem_inc(lmax_ready, 1)
                        vec.wait_ge(gmax_ready, 1)
                        link(nc.vector.tensor_tensor(spread[:], gmax[:, 0:H], gmax[:, H:2 * H], ALU.add))
                        link(nc.vector.tensor_reduce(test[:, 0:1], spread[:], AX.X, ALU.max))
                        link(nc.vector.tensor_reduce(test[:, 1:2], gmax[:], AX.X, ALU.max))
                        link(nc.vector.tensor_scalar(test[:, 0:1], test[:, 0:1], SPREAD, None, ALU.is_le))
                        link(nc.vector.tensor_scalar(test[:, 1:2], test[:, 1:2], LARGEST, None, ALU.is_le))
                        link(nc.vector.tensor_tensor(flag[:], test[:, 0:1], test[:, 1:2], ALU.mult))
            narrow = nc.values_load(flag[0:1, 0:1], min_val=0, max_val=1)
            v = dict(locals())
            with nc.If(narrow == 1):
                factored_attention(nc, sem, sb, banks, v)
            with nc.Else():
                general_attention(nc, sem, sb, banks, v)


def factored_attention(nc, sem, sb, banks, v):
    N, F, H, D, NC, NG, GW, GB, E = (v[k] for k in ("N", "F", "H", "D", "NC", "NG", "GW", "GB", "E"))
    wh, h2t, xs, w_ext, gmax = v["wh"], v["h2t"], v["xs"], v["w_ext"], v["gmax"]
    mask_dram, out_dram = v["mask_dram"], v["out_dram"]
    NP = H // 2
    C1 = D + 1
    C3 = 3 * C1
    CG = 2 * C3
    CM = 2 * C3 + 2
    CV = 4 * C3 + 2
    OB = (0, 3 * C3 + 2)
    OD = (C3, 2 * C3 + 2)
    OG = (0, 2 * C3 + 2)
    PIECE = 8
    NPC = NC // PIECE
    NGB = 8
    BIG = float(2 ** 30)
    out_view = out_dram.rearrange("(b p) f -> p b f", p=P)
    mask_view = mask_dram.rearrange("(c p) i -> p c i", p=P)
    scope = ExitStack()
    with scope:
        vals = sb("vals", [P, NC * NP, CV], BF16, scope)
        dcol = sb("dcol", [P, NC, H], F32, scope)
        ndcol = sb("ndcol", [P, NC, H], F32, scope)
        dbig = sb("dbig", [P, NC, H], F32, scope)
        amul = sb("amul", [P, NC, H], F32, scope)
        cmul = sb("cmul", [P, NC, H], F32, scope)
        mean = sb("mean", [P, F], F32, scope)
        wrep = sb("wrep2", [P, H, P], F32, scope)

        prep = ExitStack()
        with prep:
            part = sb("part", [P, NC * NP, 2, C1], F32, prep)
            bexp = sb("bexp", [P, NC, H], F32, prep)
            dexp = sb("dexp", [P, NC, H], F32, prep)
            z0 = sb("z0", [P, NC, H], F32, prep)
            z5 = sb("z5", [P, NC, H], F32, prep)
            zm = sb("zm", [P, NC, H], F32, prep)
            ones = sb("ones", [P, P], F32, prep)
            vec5, exp_in, exp_out, ones_ready, mean_ps, mean_done = (sem(n) for n in ("vec5", "exp_in", "exp_out",
                                                                     "ones_ready", "mean_ps", "mean_done"))
            full, high_done, rest_ready, mid_done, ones_col = (sem(n) for n in ("full", "high_done", "rest_ready", "mid_done", "ones_col"))
            with nc.Block() as block:
                @block.tensor
                def _(pe):
                    pe.wait_ge(ones_ready, 1)
                    for c in range(NC):
                        last = nc.tensor.matmul(banks[0][:, 0:F], ones[:], wh[:, c, 0:F], start=(c == 0), stop=(c == NC - 1))
                    last.then_inc(mean_ps, 1)

                @block.gpsimd
                def _(pool):
                    nc.gpsimd.memset(ones[:], 1.0).then_inc(ones_ready, 1)
                    nc.gpsimd.memset(vals[:, :, OD[0] + C3:OD[0] + C3 + 1], 1.0).then_inc(ones_col, 1)
                    nc.gpsimd.memset(vals[:, :, OD[0] + C3 + 1:OD[0] + C3 + 2], 0.0).then_inc(ones_col, 1)
                    pool.wait_ge(ones_col, 2)

                @block.scalar
                def _(act):
                    for n, t in enumerate((bexp, dexp, amul, cmul)):
                        act.wait_ge(exp_in, n + 1)
                        nc.scalar.activation(t[:], t[:], ACT.Exp).then_inc(exp_out, 1)
                    act.wait_ge(mean_ps, 1)
                    nc.scalar.mul(mean[:], banks[0][:, 0:F], 1.0 / N).then_inc(mean_done, 1)
                    for q, off in enumerate((OB, OD)):
                        act.wait_ge(full, q + 1)
                        for k in range(2):
                            nc.scalar.copy(vals[:, :, off[k]:off[k] + C1], part[:, :, k, :]).then_inc(high_done, 1)
                        for k in range(2):
                            act.wait_ge(rest_ready, 2 * q + k + 1)
                            nc.scalar.copy(vals[:, :, off[k] + C1:off[k] + 2 * C1], part[:, :, k, :]).then_inc(mid_done, 1)
                    act.wait_ge(mean_done, 1)

                @block.vector
                def _(vec):
                    count = [0]

                    def link(ins):
                        count[0] += 1
                        ins.then_inc(vec5, 1)
                        vec.wait_ge(vec5, count[0])

                    dmax = gmax[:, 0:H].unsqueeze(1).to_broadcast([P, NC, H])
                    link(nc.vector.tensor_copy(dcol[:], wh[:, :, F + H:E]))
                    link(nc.vector.tensor_tensor(bexp[:], dcol[:], dmax, ALU.subtract))
                    link(nc.vector.tensor_scalar(dexp[:], bexp[:], ALPHA, None, ALU.mult))
                    vec.sem_inc(exp_in, 2)
                    link(nc.vector.tensor_scalar(ndcol[:], dcol[:], -1.0, None, ALU.mult))
                    link(nc.vector.tensor_scalar(dbig[:], dcol[:], BIG, None, ALU.mult))
                    link(nc.vector.tensor_tensor(z0[:], wh[:, :, F:F + H], dmax, ALU.add))
                    link(nc.vector.tensor_scalar(z5[:], z0[:], ALPHA, None, ALU.mult))
                    link(nc.vector.tensor_tensor(zm[:], z0[:], z5[:], ALU.max))
                    link(nc.vector.tensor_tensor(amul[:], z0[:], zm[:], ALU.subtract))
                    link(nc.vector.tensor_tensor(cmul[:], z5[:], zm[:], ALU.subtract))
                    vec.sem_inc(exp_in, 2)
                    link(nc.vector.tensor_copy(wrep[:], w_ext[:, F:F + H].unsqueeze(2).to_broadcast([P, H, P])))
                    for q, (t, off) in enumerate(((bexp, OB), (dexp, OD))):
                        vec.wait_ge(exp_out, q + 1)
                        heads = part[:].rearrange("p (c a) k e -> p c (a k) e", c=NC)
                        link(nc.vector.tensor_tensor(heads[:, :, :, 0:D], wh[:, :, 0:F].rearrange("p c (h e) -> p c h e", h=H),
                                                     t[:].unsqueeze(3).to_broadcast([P, NC, H, D]), ALU.mult))
                        link(nc.vector.tensor_copy(heads[:, :, :, D:C1], t[:].unsqueeze(3)))
                        vec.sem_inc(full, 1)
                        for k in range(2):
                            vec.wait_ge(high_done, 2 * q + k + 1)
                            link(nc.vector.tensor_tensor(part[:, :, k, :], part[:, :, k, :], vals[:, :, off[k]:off[k] + C1],
                                                         ALU.subtract))
                            vec.sem_inc(rest_ready, 1)
                        for k in range(2):
                            vec.wait_ge(mid_done, 2 * q + k + 1)
                            link(nc.vector.tensor_tensor(vals[:, :, off[k] + 2 * C1:off[k] + C3], part[:, :, k, :],
                                                         vals[:, :, off[k] + C1:off[k] + 2 * C1], ALU.subtract))

        mask = sb("mask", [P, NC, GW], BF16, scope)
        srow = sb("srow", [P, H, GW], F32, scope)
        step = [sb(f"step{i}", [P, GW], BF16, scope) for i in range(4)]
        hmat = [sb(f"hmat{i}", [P, GW], BF16, scope) for i in range(NGB)]
        own = sb("own", [P, GB, 2 * CG], F32, scope)
        all_ = sb("all", [P, GB, CM], F32, scope)
        bsum = sb("bsum", [P, GB, 2, C1], F32, scope)
        dsum = sb("dsum", [P, GB, 2, C3], F32, scope)
        inv = sb("inv", [P, GB, 2], F32, scope)
        empty = sb("empty", [P, GB], F32, scope)
        o = sb("o2", [P, GB, F], F32, scope)
        neg = sb("neg2", [P, GB, F], F32, scope)

        mask_in = [sem(f"mask_in{i}") for i in range(NPC)]
        piece_free = [sem(f"piece_free{i}") for i in range(NPC - 1)]
        srow_ps, srow_ready = sem("srow_ps"), sem("srow_ready")
        step_ready = sem("step_ready")
        hmat_ready, hmat_free = sem("hmat_ready"), sem("hmat_free")
        swept, cleared, fin_free = sem("swept"), sem("cleared"), sem("fin_free")
        den_ready, inv_ready, chain, gpass = sem("den_ready"), sem("inv_ready"), sem("chain"), sem("gpass")
        neg_ready, neg_exp, o_ready, o_out = sem("neg_ready"), sem("neg_exp"), sem("o_ready2"), sem("o_out")
        vpass, apass, ppass = sem("vpass"), sem("apass"), sem("ppass")
        U = 2 * NC

        def by_act(c, k):
            return k == 1

        with nc.Block() as block:
            @block.sync
            def _(sp):
                def load(g, p):
                    sp.dma_start(mask[:, p * PIECE:(p + 1) * PIECE, :],
                                 mask_view[:, p * PIECE:(p + 1) * PIECE, bass.ts(g, GW)]).then_inc(mask_in[p], 16)
                for p in range(NPC):
                    load(0, p)
                with sp.Fori(1, NG) as g:
                    for p in range(NPC):
                        if p < NPC - 1:
                            sp.wait_ge(piece_free[p], g)
                        else:
                            sp.wait_ge(swept, NP * g)
                        load(g, p)
                    sp.wait_ge(o_ready, g)
                    sp.dma_start(out_view[:, bass.ts(g - 1, GB), :], o[:]).then_inc(o_out, 16)
                sp.wait_ge(o_ready, NG)
                sp.dma_start(out_view[:, (NG - 1) * GB:NG * GB, :], o[:]).then_inc(o_out, 16)
                sp.wait_ge(o_out, 16 * NG)

            @block.tensor
            def _(pe):
                def rows(g, a, static=False):
                    for k in range(2):
                        src = h2t[:, g * GW:(g + 1) * GW] if static else h2t[:, bass.ts(g, GW)]
                        nc.tensor.matmul(banks[6 + k][:], wrep[:, 2 * a + k, :], src, start=True, stop=True).then_inc(srow_ps, 1)

                def sweep(g, a, s, ahead):
                    for c in range(NC):
                        for k in range(2):
                            pe.wait_ge(hmat_ready, U * s + 2 * c + k + 1)
                            m = hmat[(2 * c + k) % NGB]
                            for b in range(GB):
                                if c == 0 and k == 0:
                                    pe.wait_ge(cleared, 6 * s + b + 1)
                                last = nc.tensor.matmul(banks[b][:, k * CG:(k + 1) * CG], m[:, b * P:(b + 1) * P],
                                                        vals[:, NP * c + a, OG[k]:OG[k] + CG], start=(c == 0 and k == 0),
                                                        stop=(c == NC - 1), skip_group_check=True)
                            last.then_inc(hmat_free, 1)
                        for b in range(GB):
                            if c == 0 and b % 2 == 0:
                                pe.wait_ge(cleared, 6 * s + 4 + b // 2 + 1)
                            last = nc.tensor.matmul(banks[4 + b // 2][:, b % 2 * CM:(b % 2 + 1) * CM],
                                                    mask[:, c, b * P:(b + 1) * P], vals[:, NP * c + a, OD[0]:OD[0] + CM],
                                                    start=(c == 0 and b % 2 == 0), stop=(c == NC - 1), skip_group_check=True)
                        if c == NC - 1:
                            last.then_inc(swept, 1)
                        elif a == NP - 1 and c % PIECE == PIECE - 1:
                            last.then_inc(piece_free[c // PIECE], 1)
                        if c == 20:
                            ahead()

                for a in range(NP):
                    rows(0, a, True)
                    pe.wait_ge(srow_ready, 2 * (a + 1))
                with pe.Fori(0, NG - 1) as g:
                    sweep(g, 0, 2 * g, lambda: None)

                    def both():
                        pe.wait_ge(srow_ready, 2 * NP * (g + 1))
                        rows(g + 1, 0)
                    sweep(g, 1, 2 * g + 1, both)
                    pe.wait_ge(srow_ready, 2 * NP * (g + 1) + 2)
                    rows(g + 1, 1)
                sweep(NG - 1, 0, 2 * (NG - 1), lambda: None)
                sweep(NG - 1, 1, 2 * (NG - 1) + 1, lambda: None)

            @block.scalar
            def _(act):
                act.sem_inc(cleared, 6)

                def rows(g, a, s, first=False):
                    for k in range(2):
                        act.wait_ge(srow_ps, 2 * s + k + 1)
                        if k == 0 and not first:
                            act.wait_ge(hmat_ready, U * (s - 1))
                        nc.scalar.copy(srow[:, 2 * a + k, :], banks[6 + k][:]).then_inc(srow_ready, 1)

                def steps(s, a, c, k, first):
                    if not first or c >= 4:
                        act.wait_ge(hmat_ready, U * s + 2 * c - 6)
                    nc.scalar.activation(step[c % 4][:], srow[:, 2 * a + k, :], ACT.Relu, bias=dbig[:, c, 2 * a + k:2 * a + k + 1],
                                         scale=BIG).then_inc(step_ready, 1)

                def clear(s):
                    act.wait_ge(fin_free, s + 1)
                    hold(act, swept, s + 1, apass)
                    for b in range(GB):
                        nc.scalar.copy(own[:, b, :], banks[b][:, 0:2 * CG]).then_inc(cleared, 1)
                    for b in range(2):
                        nc.scalar.copy(all_[:, 2 * b:2 * b + 2, :],
                                       banks[4 + b][:, 0:2 * CM].rearrange("p (b e) -> p b e", e=CM)).then_inc(cleared, 1)

                def sweep(g, a, s, first=False):
                    for c in range(NC):
                        if c == 3 and not first:
                            clear(s - 1)
                        steps(s, a, c, 1, first)

                def elu(g):
                    act.wait_ge(neg_ready, g + 1)
                    nc.scalar.activation(neg[:], neg[:], ACT.Exp).then_inc(neg_exp, 1)

                for a in range(NP):
                    rows(0, a, a, True)
                sweep(0, 0, 0, True)
                sweep(0, 1, 1)
                rows(1, 0, 2)
                rows(1, 1, 3)
                with act.Fori(1, NG) as g:
                    sweep(g, 0, 2 * g)
                    elu(g - 1)
                    sweep(g, 1, 2 * g + 1)
                    with act.If(g < NG - 1):
                        rows(g + 1, 0, 2 * g + 2)
                        rows(g + 1, 1, 2 * g + 3)
                clear(2 * NG - 1)
                elu(NG - 1)

            @block.vector
            def _(vec):
                def sweep(g, a, s, first=False):
                    vec.wait_ge(srow_ready, 2 * (s + 1))
                    for c in range(NC):
                        if a == 0 and c % PIECE == 0:
                            vec.wait_ge(mask_in[c // PIECE], 16 * (g + 1))
                        for k in range(2):
                            n = U * s + 2 * c + k
                            if not first or 2 * c + k >= NGB:
                                vec.wait_ge(hmat_free, n + 1 - NGB)
                            m = hmat[(2 * c + k) % NGB]
                            if k == 1:
                                vec.wait_ge(step_ready, NC * s + c + 1)
                                nc.vector.tensor_tensor(m[:], step[c % 4][:], mask[:, c, :], ALU.min).then_inc(hmat_ready, 1)
                            else:
                                nc.vector.scalar_tensor_tensor(m[:], srow[:, 2 * a + k, :], ndcol[:, c, 2 * a + k:2 * a + k + 1],
                                                               mask[:, c, :], ALU.is_gt, ALU.mult).then_inc(hmat_ready, 1)
                        if c == 12 and not first:
                            invert(s - 1)

                def invert(s):
                    vec.wait_ge(den_ready, s + 1)
                    nc.vector.reciprocal(inv[:], bsum[:, :, :, D]).then_inc(inv_ready, 1)

                sweep(0, 0, 0, True)
                sweep(0, 1, 1)
                with vec.Fori(1, NG) as g:
                    sweep(g, 0, 2 * g)
                    sweep(g, 1, 2 * g + 1)
                invert(2 * NG - 1)

            @block.gpsimd
            def _(pool):
                pool.sem_inc(fin_free, 1)
                total = [0]

                def finish(g, a, s, base, static):
                    def link(ins):
                        total[0] += 1
                        ins.then_inc(chain, 1)
                        hold(pool, chain, base + total[0], ppass) if not static else pool.wait_ge(chain, base + total[0])
                    pool.wait_ge(cleared, 6 * (s + 2)) if static else hold(pool, cleared, 6 * (s + 2), ppass)
                    amul_g = (amul[:, g * GB:(g + 1) * GB, :] if static else amul[:, bass.ts(g, GB), :])
                    cmul_g = (cmul[:, g * GB:(g + 1) * GB, :] if static else cmul[:, bass.ts(g, GB), :])
                    for k in range(2):
                        h = 2 * a + k
                        ob = OB[k] if k == 0 else OB[k] - 2
                        od = OD[k] if k == 0 else OD[k] - 2
                        md = k * (C3 + 2)
                        bs, ds = bsum[:, :, k, :], dsum[:, :, k, :]
                        link(nc.gpsimd.tensor_tensor(bs, own[:, :, ob + 2 * C1:ob + C3], own[:, :, ob + C1:ob + 2 * C1], ALU.add))
                        link(nc.gpsimd.tensor_tensor(bs, bs, own[:, :, ob:ob + C1], ALU.add))
                        link(nc.gpsimd.tensor_tensor(ds, all_[:, :, md:md + C3], own[:, :, od:od + C3], ALU.subtract))
                        link(nc.gpsimd.tensor_tensor(ds[:, :, 0:C1], ds[:, :, 0:C1], ds[:, :, C1:2 * C1], ALU.add))
                        link(nc.gpsimd.tensor_tensor(ds[:, :, 0:C1], ds[:, :, 0:C1], ds[:, :, 2 * C1:C3], ALU.add))
                        link(nc.gpsimd.tensor_tensor(bs, bs, amul_g[:, :, h:h + 1].to_broadcast([P, GB, C1]), ALU.mult))
                        link(nc.gpsimd.tensor_tensor(ds[:, :, 0:C1], ds[:, :, 0:C1],
                                                     cmul_g[:, :, h:h + 1].to_broadcast([P, GB, C1]), ALU.mult))
                        link(nc.gpsimd.tensor_tensor(bs, bs, ds[:, :, 0:C1], ALU.add))
                    link(nc.gpsimd.tensor_scalar(empty[:], all_[:, :, C3], 0.0, None, ALU.is_equal))
                    for k in range(2):
                        h = 2 * a + k
                        link(nc.gpsimd.tensor_tensor(bsum[:, :, k, D], bsum[:, :, k, D], empty[:], ALU.add))
                        link(nc.gpsimd.tensor_tensor(dsum[:, :, k, 0:D], empty[:].unsqueeze(2).to_broadcast([P, GB, D]),
                                                     mean[:, h * D:(h + 1) * D].unsqueeze(1).to_broadcast([P, GB, D]), ALU.mult))
                        link(nc.gpsimd.tensor_tensor(bsum[:, :, k, 0:D], bsum[:, :, k, 0:D], dsum[:, :, k, 0:D], ALU.add))
                    pool.sem_inc(den_ready, 1)
                    pool.sem_inc(fin_free, 1)
                    pool.wait_ge(inv_ready, s + 1) if static else hold(pool, inv_ready, s + 1, ppass)
                    for k in range(2):
                        h = 2 * a + k
                        link(nc.gpsimd.tensor_tensor(o[:, :, h * D:(h + 1) * D], bsum[:, :, k, 0:D],
                                                     inv[:, :, k:k + 1].to_broadcast([P, GB, D]), ALU.mult))

                def output(g, base, static):
                    def link(ins):
                        total[0] += 1
                        ins.then_inc(chain, 1)
                        hold(pool, chain, base + total[0], ppass) if not static else pool.wait_ge(chain, base + total[0])
                    link(nc.gpsimd.tensor_scalar(neg[:], o[:], 0.0, None, ALU.min))
                    pool.sem_inc(neg_ready, 1)
                    xsg = xs[:, g * GB:(g + 1) * GB, :] if static else xs[:, bass.ts(g, GB), :]
                    link(nc.gpsimd.tensor_scalar(o[:], o[:], 0.0, -1.0, ALU.max, ALU.add))
                    link(nc.gpsimd.tensor_tensor(o[:], o[:], xsg, ALU.add))
                    pool.wait_ge(neg_exp, g + 1) if static else hold(pool, neg_exp, g + 1, ppass)
                    link(nc.gpsimd.tensor_tensor(o[:], o[:], neg[:], ALU.add))
                    pool.sem_inc(o_ready, 1)

                finish(0, 0, 0, 0, True)
                finish(0, 1, 1, 0, True)
                output(0, 0, True)
                LPG = total[0]
                with pool.Fori(1, NG) as g:
                    total[0] = 0
                    hold(pool, o_out, 16 * g, ppass)
                    finish(g, 0, 2 * g, LPG * g, False)
                    finish(g, 1, 2 * g + 1, LPG * g, False)
                    output(g, LPG * g, False)





def general_attention(nc, sem, sb, banks, v):
    N, F, H, D, NC, NG, GW, GB, E = (v[k] for k in ("N", "F", "H", "D", "NC", "NG", "GW", "GB", "E"))
    wh, h2t, xs, ident, w_ext = v["wh"], v["h2t"], v["xs"], v["ident"], v["w_ext"]
    adj_rows, out_rows = v["adj_rows"], v["out_rows"]
    scope = ExitStack()
    with scope:
        wrep = sb("wrep", [P, H, P], F32, scope)
        drow = sb("drow", [P, H, N], F32, scope)
        arow = sb("arow", [P, N], I32, scope)
        keep = sb("keep", [P, N], F32, scope)
        fill = sb("fill", [P, N], F32, scope)
        e = sb("e", [P, N], F32, scope)
        pt = arow[:].bitcast(F32)
        ssrc = sb("ssrc", [P, H], F32, scope)
        nmax = sb("nmax", [P, 1], F32, scope)
        den = sb("den", [P, H], F32, scope)
        rden = sb("rden", [P, 1], F32, scope)
        o = sb("o", [P, F], F32, scope)
        neg = sb("neg", [P, F], F32, scope)
        wrep_ready, drow_ps, drow_done = sem("wrep_ready"), sem("drow_ps"), sem("drow_done")
        arow_in, arow_free, e_ready, p_ready, p_ps, p_evac, pv, vec3, s_elu, elu_exp, o_ready, stored = (
            sem(n) for n in ("arow_in", "arow_free", "e_ready", "p_ready", "p_ps", "p_evac", "pv", "vec3", "s_elu",
                             "elu_exp", "o_ready", "stored"))
        VL = 3 + 6 * H + 3
        with nc.Block() as block:
            @block.sync
            def _(sp):
                with sp.Fori(0, NC) as b:
                    sp.wait_ge(arow_free, b + 1)
                    sp.dma_start(arow[:], adj_rows[b]).then_inc(arow_in, 16)
                    sp.wait_ge(o_ready, b + 1)
                    sp.dma_start(out_rows[b], o[:]).then_inc(stored, 16)
                sp.wait_ge(stored, 16 * NC)

            @block.tensor
            def _(pe):
                pe.wait_ge(wrep_ready, 1)
                for h in range(H):
                    for g in range(NG):
                        n = NG * h + g
                        if n >= 4:
                            pe.wait_ge(drow_done, n - 3)
                        nc.tensor.matmul(banks[n % 4][:], wrep[:, h, :], h2t[:, g * GW:(g + 1) * GW],
                                         start=True, stop=True).then_inc(drow_ps, 1)
                pe.wait_ge(drow_done, NG * H)
                with pe.Fori(0, NC) as b:
                    for h in range(H):
                        i = b * H + h
                        pe.wait_ge(p_ready, i + 1)
                        for g in range(NG):
                            if g >= 2:
                                pe.wait_ge(p_evac, NG * i + g - 1)
                            for k in range(GB):
                                c = GB * g + k
                                last = nc.tensor.transpose(banks[g % 2][:, k * P:(k + 1) * P], e[:, c * P:(c + 1) * P],
                                                           ident[:])
                            last.then_inc(p_ps, 1)
                        pe.wait_ge(p_evac, NG * (i + 1))
                        for c in range(NC):
                            last = nc.tensor.matmul(banks[2 + h][:, 0:D], pt[:, c * P:(c + 1) * P],
                                                    wh[:, c, h * D:(h + 1) * D], start=(c == 0), stop=(c == NC - 1))
                        last.then_inc(pv, 1)

            @block.scalar
            def _(act):
                for n in range(NG * H):
                    act.wait_ge(drow_ps, n + 1)
                    nc.scalar.copy(drow[:, n // NG, (n % NG) * GW:(n % NG + 1) * GW], banks[n % 4][:]).then_inc(drow_done, 1)
                with act.Fori(0, NC) as b:
                    for h in range(H):
                        i = b * H + h
                        act.wait_ge(e_ready, i + 1)
                        nc.scalar.activation(e[:], e[:], ACT.Exp, bias=nmax[:, 0:1], scale=1.0,
                                             accum_out=den[:, h:h + 1]).then_inc(p_ready, 1)
                        for g in range(NG):
                            act.wait_ge(p_ps, NG * i + g + 1)
                            if h > 0 and g == 0:
                                act.wait_ge(pv, i)
                            nc.scalar.copy(pt[:, g * GW:(g + 1) * GW], banks[g % 2][:]).then_inc(p_evac, 1)
                    act.wait_ge(s_elu, b + 1)
                    nc.scalar.activation(neg[:], neg[:], ACT.Exp).then_inc(elu_exp, 1)

            @block.vector
            def _(vec):
                nc.vector.tensor_copy(wrep[:], w_ext[:, F + H:E].unsqueeze(2).to_broadcast([P, H, P])).then_inc(wrep_ready, 1)
                vec.wait_ge(drow_done, NG * H)
                vec.sem_inc(arow_free, 1)
                with vec.Fori(0, NC) as b:
                    count = [0]

                    def link(ins):
                        count[0] += 1
                        ins.then_inc(vec3, 1)
                        vec.wait_ge(vec3, VL * b + count[0])
                    vec.wait_ge(arow_in, 16 * (b + 1))
                    link(nc.vector.tensor_scalar(keep[:], arow[:], 0.0, None, ALU.is_gt))
                    link(nc.vector.tensor_scalar(fill[:], keep[:], 1.0, NEG_INF, ALU.subtract, ALU.mult))
                    link(nc.vector.tensor_copy(ssrc[:], wh[:, bass.ds(b, 1), F:F + H].rearrange("p o e -> p (o e)")))
                    for h in range(H):
                        i = b * H + h
                        if h > 0:
                            vec.wait_ge(p_evac, NG * i)
                        link(nc.vector.tensor_scalar(e[:], drow[:, h, :], ssrc[:, h:h + 1], None, ALU.add))
                        link(nc.vector.scalar_tensor_tensor(e[:], e[:], ALPHA, e[:], ALU.mult, ALU.max))
                        link(nc.vector.tensor_tensor(e[:], e[:], keep[:], ALU.mult))
                        link(nc.vector.tensor_tensor(e[:], e[:], fill[:], ALU.add))
                        link(nc.vector.tensor_reduce(nmax[:], e[:], AX.X, ALU.max, negate=True))
                        vec.sem_inc(e_ready, 1)
                        vec.wait_ge(p_ready, i + 1)
                        link(nc.vector.reciprocal(rden[:], den[:, h:h + 1]))
                        vec.wait_ge(pv, i + 1)
                        ins = nc.vector.tensor_scalar(o[:, h * D:(h + 1) * D], banks[2 + h][:, 0:D], rden[:, 0:1], None,
                                                      ALU.mult)
                    ins.then_inc(arow_free, 1)
                    vec.wait_ge(arow_free, b + 2)
                    nc.vector.tensor_scalar(neg[:], o[:], 0.0, None, ALU.min).then_inc(s_elu, 1)
                    vec.wait_ge(elu_exp, b + 1)
                    link(nc.vector.tensor_scalar(o[:], o[:], 0.0, None, ALU.max))
                    link(nc.vector.scalar_tensor_tensor(o[:], neg[:], -1.0, o[:], ALU.add, ALU.add))
                    link(nc.vector.tensor_tensor(o[:], o[:], xs[:, bass.ds(b, 1), :].rearrange("p o f -> p (o f)"), ALU.add))
                    vec.sem_inc(o_ready, 1)
                    vec.wait_ge(stored, 16 * (b + 1))


_INS = ["x", "adj", "L1_gnn_W", "L1_gnn_a"]


def kernel(**inputs):
    import numpy as _np
    import concourse.bacc as _bacc
    from concourse import mybir as _mybir
    from concourse.bass_utils import run_bass_kernel_spmd as _run

    nc = _bacc.Bacc("TRN2", target_bir_lowering=False, num_devices=1)
    arrays, args = {}, []
    for name in _INS:
        a = _np.ascontiguousarray(inputs[name])
        arrays[f"in_{name}"] = a
        args.append(nc.dram_tensor(f"in_{name}", a.shape, _mybir.dt.from_np(a.dtype), kind="ExternalInput").ap())
    out = nc.dram_tensor("out_x", inputs["x"].shape, _mybir.dt.float32, kind="ExternalOutput").ap()
    emit(nc, *args, out)
    r = _run(nc, [arrays], core_ids=[0])
    return r.results[0]["out_x"]
```

```python
import concourse.bass as bass
from concourse import mybir
from contextlib import ExitStack

F32 = mybir.dt.float32
BF16 = mybir.dt.bfloat16
F16 = mybir.dt.float16
I32 = mybir.dt.int32
ALU = mybir.AluOpType
ACT = mybir.ActivationFunctionType
AX = mybir.AxisListType

P = 128
WIN = 4
DIAG = 512.0
SCALE = 4096.0
EPS = 1e-5
ALPHA = 0.2
NEG_INF = 9000000000000000.0
SPREAD = 60.0
LARGEST = 1e6


def hold(engine, semaphore, value, passed):
    engine.wait_ge(semaphore, value)
    engine.sem_inc(passed, 1)


def emit(nc, x_dram, adj_dram, w_dram, a_dram, out_dram):
    N, F = x_dram.shape
    H, D2 = a_dram.shape[1], a_dram.shape[2]
    D = D2 // 2
    NC = N // P
    GW = 512
    NG = N // GW
    GB = GW // P
    E = F + 2 * H
    adj_view = adj_dram.rearrange("(g b p) (w j) -> w g p b j", p=P, b=GB, j=WIN * P)
    adj_tiles = lambda w, g: adj_view[w, g]
    adj_rows = adj_dram.rearrange("(b p) j -> b p j", p=P)
    x_view = x_dram.rearrange("(b p) f -> p b f", p=P)
    mask_dram = nc.dram_tensor("mask_t_dram", (N, N), BF16, kind="Internal").ap()
    mask_parts = mask_dram.rearrange("(w q p) (g i) -> w g p q i", p=P, q=WIN, i=GW)
    mask_tiles = lambda w, g: mask_parts[w, g]
    out_rows = out_dram.rearrange("(b p) f -> b p f", p=P)
    s_dram = nc.dram_tensor("s_dram", (H, N), F32, kind="Internal").ap()

    ctx = ExitStack()

    def sem(name):
        return ctx.enter_context(nc.semaphore(name))

    with ctx:
        def sb(name, shape, dt, where=ctx):
            return where.enter_context(nc.sbuf_tensor(name, shape, dt))

        banks = [ctx.enter_context(nc.psum_tensor(f"bank{i}", [P, 512], F32)) for i in range(8)]

        ident = sb("ident", [P, P], F32)
        xs = sb("xs", [P, NC, F], F32)
        w_ext = sb("w_ext", [P, E], F32)
        acc = sb("acc", [P, N], F32)
        stats = sb("stats", [P, NC, 6], F32)
        mv = sb("mv", [P, NC, 2], F32)
        rstd = sb("rstd", [P, NC], F32)
        vareps = sb("vareps", [P, NC], F32)
        wt = sb("wt", [P, P], F32)
        a_diag = sb("a_diag", [P, 2 * H], F32)
        w_in, a_in, a_zero = sem("w_in"), sem("a_in"), sem("a_zero")

        def statistics(vec, link, blocks, sqrt_in_ready, sqrt_done, count):
            r = slice(blocks.start, blocks.stop)
            for b in blocks:
                last = nc.vector.bn_stats(stats[:, b, :], xs[:, b, :])
            link(last)
            for b in blocks:
                last = nc.vector.bn_aggr(mv[:, b, :], stats[:, b, :])
            link(last)
            nc.vector.tensor_scalar(rstd[:, r], mv[:, r, 1], EPS, None, ALU.add).then_inc(sqrt_in_ready, 1)
            link(nc.vector.tensor_scalar(vareps[:, r], mv[:, r, 1], EPS, -0.5, ALU.add, ALU.mult))
            vec.wait_ge(sqrt_done, count)
            link(nc.vector.reciprocal(rstd[:, r], rstd[:, r]))
            link(nc.vector.tensor_tensor(vareps[:, r], vareps[:, r], rstd[:, r], ALU.mult))
            link(nc.vector.tensor_tensor(vareps[:, r], vareps[:, r], rstd[:, r], ALU.mult))
            link(nc.vector.scalar_tensor_tensor(rstd[:, r], vareps[:, r], 1.5, rstd[:, r], ALU.add, ALU.mult))

        def linker(vec, s):
            count = [0]

            def link(ins):
                count[0] += 1
                ins.then_inc(s, 1)
                vec.wait_ge(s, count[0])
            return link

        first = ExitStack()
        with first:
            ident16 = sb("ident16", [P, P], BF16, first)
            rank_w = sb("rank_w", [P, P], BF16, first)
            rank_rest = sb("rank_rest", [P, P], F16, first)
            count_rest = sb("count_rest", [P, P], F16, first)
            h_ready = sem("h_ready")
            hparts = sb("hparts", [P, NC, 2, F], F16, first)
            adjs = [sb(f"adjs{i}", [P, GB, WIN * P], I32, first) for i in range(2)]
            adj_in = [sem(f"adj_in{i}") for i in range(2)]

            scope = ExitStack()
            with scope:
                adj16 = [sb(f"adj16_{q}", [P, GW], BF16, scope) for q in range(WIN)]
                mask_t = [sb(f"mask_t{s}", [P, WIN, GW], BF16, scope) for s in range(2)]
                code = [sb(f"code{i}", [P, GW], F16, scope) for i in range(2)]
                rest_code = sb("rest_code", [P, 2 * NG, WIN, GW], F16, scope)
                pick = [[sb(f"pick{i}_{r}", [P, GW], F16, scope) for r in range(2)] for i in range(2)]
                rest = [sb(f"rest{q}", [P, GW], F16, scope) for q in range(WIN)]
                rest_pick = [[sb(f"rest_pick{i}_{r}", [P, GW], F16, scope) for r in range(2)] for i in range(2)]
                over_pick = sb("over_pick", [P, WIN, GW], F16, scope)
                last_row = sb("last_row", [P, N // P], F16, scope)
                minus = sb("minus", [P, N // P], F32, scope)
                rowmax = sb("rowmax", [P, 1], F32, scope)
                maxrow = sb("maxrow", [1, P], F32, scope)
                top = sb("top", [1, NG], F32, scope)
                top_count = sb("top_count", [1, NG], I32, scope)
                bit = sb("bit", [1, 2, NG], F32, scope)
                needy = sb("needy", [1, 2, NG], F32, scope)
                need = sb("need", [1, 1], I32, scope)
                hc = sb("hc", [P, F], F32, scope)
                h = sb("h", [P, WIN, F], F32, scope)
                want = sb("want", [P, 1], F32, scope)

                adj16_ready, turned, mask_ready = sem("adj16_ready"), sem("turned"), sem("mask_ready")
                coded, code_ready, pick_ready = sem("coded"), sem("code_ready"), sem("pick_ready")
                gathered, maxed = sem("gathered"), sem("maxed")
                rest_coded, rest_code_ready = sem("rest_coded"), sem("rest_code_ready")
                rest_pick_ready, rest_gathered, rest_maxed = sem("rest_pick_ready"), sem("rest_gathered"), sem("rest_maxed")
                mask_out = [sem(f"mask_out{s}") for s in range(2)]
                last_in, maxrow_in = sem("last_in"), sem("maxrow_in")
                rest_ready, norm = sem("rest_ready"), sem("norm")
                over_pick_ready, over_gathered, over_maxed = sem("over_pick_ready"), sem("over_gathered"), sem("over_maxed")
                bit_set = sem("bit_set")
                want_set, slot_free, stat = sem("want_set"), sem("slot_free"), sem("stat")
                pool_passed, pe_passed, vec_passed, act_passed = (sem("pool_passed"), sem("pe_passed"),
                                                                  sem("vec_passed"), sem("act_passed"))

                turn_ps = [banks[i][:, 0:GW // 2].bitcast(BF16) for i in range(2)]
                code_ps, rest_code_ps = banks[2], banks[3]
                near_ps, rest_ps = banks[4:6], banks[6:8]
                x_in, x_rest_in = sem("x_in"), sem("x_rest_in")
                norm_chain, const_built, ident_built, rank_built = (sem("norm_chain"), sem("const_built"),
                                                                    sem("ident_built"), sem("rank_built"))
                acc_zero, var_ready, sqrt_done, rstd_ready = (sem("acc_zero"), sem("var_ready"), sem("sqrt_done"),
                                                              sem("rstd_ready"))
                NU = NG * NC // WIN
                NV = NU // 2
                STEPS = WIN * NU

                def at(t, i, n):
                    return t[:, i * n:(i + 1) * n] if isinstance(i, int) else t[:, bass.ts(i, n)]

                def wait(engine, semaphore, value):
                    if not isinstance(value, int) or value > 0:
                        engine.wait_ge(semaphore, value)

                LATE = NG + 2
                FREE = NG

                def late(u):
                    return (u + NU - LATE) % NU

                def walk(engine, pair, count, load):
                    nothing = lambda s, q: None
                    pair(0, nothing)
                    with engine.Fori(0, NG - 1) as w:
                        with engine.Fori(0, NG // 2 - 1) as k:
                            pair(1 + (NG // 2) * w + k, nothing)
                        pair((NG // 2) * (w + 1), lambda s, q: count(w, s, q))
                        load(w)
                    with engine.Fori(NV - 3, NV - 1) as v:
                        pair(v, nothing)
                    pair(NV - 1, nothing)

                def leftover_beside(v):
                    return not (isinstance(v, int) and v == 0)

                def leftovers(engine, bits, which, first, more):
                    with engine.If(bits % 2 == 1):
                        first()
                        if more is not None:
                            with engine.If((bits // MORE) % 2 == 1):
                                count_left = engine.value_load(which, min_val=0, max_val=WIN * P)
                                more(count_left)
                MORE = 2 ** NG

                with nc.Block() as block:
                    @block.sync
                    def _(sp):
                        def pair(v, between):
                            last = isinstance(v, int) and v == NV - 1
                            for s in range(2):
                                u = 2 * v + s
                                if not last:
                                    sp.wait_ge(adj16_ready, WIN * (u + 1))
                                    nxt = u + 2
                                    sp.dma_start(adjs[s][:], adj_tiles(nxt // NG, nxt % NG)).then_inc(adj_in[s], 16)
                                between(s, 0)
                                sp.wait_ge(mask_ready, WIN * (u + 1))
                                sp.dma_start(mask_tiles(u // NG, u % NG), mask_t[s][:]).then_inc(mask_out[s], 16)

                        def count(w, s, q):
                            if s == 0:
                                sp.wait_ge(rest_code_ready, WIN * NG * (w + 1))
                                for g in range(NG):
                                    slot = w % 2 * NG + g
                                    src = rest_code[P - 1:P, slot, WIN - 1, :] if isinstance(slot, int) else \
                                        rest_code[P - 1:P, bass.ds(slot, 1), WIN - 1, :].rearrange("p o i -> p (o i)")
                                    sp.dma_start(last_row[g * P // NG:(g + 1) * P // NG, :], src).then_inc(last_in, 16)
                            else:
                                sp.wait_ge(stat, 9 * w + 3)
                                sp.dma_start(maxrow[:], rowmax[:]).then_inc(maxrow_in, 16)
                        sp.dma_start(xs[:, 0:WIN, :], x_view[:, 0:WIN, :]).then_inc(x_in, 16)
                        sp.dma_start(adjs[0][:], adj_tiles(0, 0)).then_inc(adj_in[0], 16)
                        sp.dma_start(xs[:, WIN:NC, :], x_view[:, WIN:NC, :]).then_inc(x_rest_in, 16)
                        sp.dma_start(adjs[1][:], adj_tiles(0, 1)).then_inc(adj_in[1], 16)
                        sp.dma_start(w_ext[:, 0:F], w_dram).then_inc(w_in, 16)
                        sp.wait_ge(a_zero, 1)
                        for k in range(2):
                            for hd in range(H):
                                sp.dma_start(a_diag[hd * D:(hd + 1) * D, k * H + hd:k * H + hd + 1],
                                             a_dram[0, hd, k * D:(k + 1) * D].unsqueeze(1)).then_inc(a_in, 16)
                        walk(sp, pair, count, lambda w: None)
                        for s in range(2):
                            count(NG - 1, s, 0)
                        for s in range(2):
                            sp.wait_ge(mask_out[s], 16 * NV)

                    @block.scalar
                    def _(act):
                        def convert(v, s, q):
                            n = WIN * (2 * v + s) + q
                            if q == 0:
                                act.wait_ge(adj_in[s], 16 * (v + 1))
                            wait(act, turned, n - WIN + 1)
                            nc.scalar.copy(adj16[q][:], adjs[s][:, :, q * P:(q + 1) * P]).then_inc(adj16_ready, 1)

                        def mask_out_of_psum(v, s, q):
                            n = WIN * (2 * v + s) + q
                            if q == 0:
                                wait(act, mask_out[s], 16 * v)
                            act.wait_ge(turned, n + 1)
                            nc.scalar.copy(mask_t[s][:, q, :], turn_ps[q % 2]).then_inc(mask_ready, 1)

                        def code_out_of_psum(v, s, q):
                            n = WIN * (2 * v + s) + q
                            wait(act, pick_ready, 2 * (n - 1))
                            wait(act, rest_ready, n - 1)
                            act.wait_ge(coded, n + 1)
                            nc.scalar.copy(code[q % 2][:], code_ps[:]).then_inc(code_ready, 1)

                        def rest_code_out_of_psum(v, s, q):
                            u = 2 * v + s
                            if q == 0:
                                act.wait_ge(slot_free, u + 1)
                            act.wait_ge(rest_coded, WIN * u + q + 1)
                            slot = u % (2 * NG)
                            dst = rest_code[:, slot, q, :] if isinstance(slot, int) else \
                                rest_code[:, bass.ds(slot, 1), q, :].rearrange("p o i -> p (o i)")
                            nc.scalar.copy(dst, rest_code_ps[:]).then_inc(rest_code_ready, 1)

                        def later(fn, v, s, q, by):
                            k = WIN * s + q + by
                            if not (isinstance(v, int) and v == NV - 1 and k >= 2 * WIN):
                                fn(v + k // (2 * WIN), k // WIN % 2, k % WIN)

                        def pair(v, between):
                            for s in range(2):
                                for q in range(WIN):
                                    later(convert, v, s, q, 3)
                                    later(mask_out_of_psum, v, s, q, 2)
                                    later(code_out_of_psum, v, s, q, 1)
                                    rest_code_out_of_psum(v, s, q)
                        def sqrt(k, blocks):
                            act.wait_ge(var_ready, k + 1)
                            nc.scalar.activation(rstd[:, blocks], rstd[:, blocks], ACT.Sqrt).then_inc(sqrt_done, 1)
                        sqrt(0, slice(0, WIN))
                        for q in range(3):
                            convert(0, 0, q)
                        mask_out_of_psum(0, 0, 0)
                        mask_out_of_psum(0, 0, 1)
                        code_out_of_psum(0, 0, 0)
                        sqrt(1, slice(WIN, NC))
                        walk(act, pair, lambda w, s, q: None, lambda w: None)

                    @block.tensor
                    def _(pe):
                        n_over = pe.alloc_register("pe_over")
                        pe.reg_mov(n_over, 0)
                        bits = pe.alloc_register("pe_bits")
                        pe.reg_mov(bits, 0)

                        def weights(u, q, k):
                            c = (u // NG) * WIN + q
                            return hparts[:, c, k, :] if isinstance(c, int) else \
                                hparts[:, bass.ds(c, 1), k, :].rearrange("p o f -> p (o f)")

                        def turn(v, s, q):
                            n = WIN * (2 * v + s) + q
                            pe.wait_ge(adj16_ready, n + 1)
                            wait(pe, mask_ready, n - 1)
                            for b in range(GB):
                                last = nc.tensor.transpose(turn_ps[q % 2][:, b * P:(b + 1) * P],
                                                           adj16[q][:, b * P:(b + 1) * P], ident16[:])
                            last.then_inc(turned, 1)

                        def make_code(v, s, q):
                            n = WIN * (2 * v + s) + q
                            pe.wait_ge(mask_ready, n + 1)
                            wait(pe, code_ready, n)
                            nc.tensor.matmul(code_ps[:], rank_w[:], mask_t[s][:, q, :], start=True, stop=True).then_inc(coded, 1)

                        def make_rest_code(v, s, q):
                            n = WIN * (2 * v + s) + q
                            pe.wait_ge(rest_ready, n + 1)
                            wait(pe, rest_code_ready, n)
                            if q > 0:
                                nc.tensor.matmul(rest_code_ps[:], count_rest[:], rest[q - 1][:], start=False, stop=False,
                                                 skip_group_check=True)
                            nc.tensor.matmul(rest_code_ps[:], rank_rest[:], rest[q][:], start=(q == 0), stop=True,
                                             skip_group_check=True).then_inc(rest_coded, 1)

                        def near(v, s, q, r):
                            u = 2 * v + s
                            n = WIN * u + q
                            pe.wait_ge(pick_ready, 2 * n + r + 1)
                            if q == 0 and r == 0 and s == 0:
                                pe.wait_ge(h_ready, WIN * (u // NG + 1))
                            wait(pe, maxed, 2 * n + r - 1)
                            if q == 3 and r == 0 and leftover_beside(v):
                                taken = pe.snap(n_over)
                                hold(pe, over_maxed, taken + 1, pe_passed)
                            for k in range(2):
                                last = nc.tensor.matmul(near_ps[r][:], weights(u, q, k), pick[q % 2][r][:],
                                                        start=(k == 0), stop=(k == 1))
                            last.then_inc(gathered, 1)

                        def fetch_leftover(chunk):
                            before = pe.snap(n_over)
                            hold(pe, over_maxed, before + 1, pe_passed)
                            pe.wait_ge(over_pick_ready, before + 1)
                            for q in range(WIN):
                                for k in range(2):
                                    w_q = hparts[:, chunk + q, k, :] if isinstance(chunk, int) else \
                                        hparts[:, bass.ds(chunk + q, 1), k, :].rearrange("p o f -> p (o f)")
                                    last = nc.tensor.matmul(near_ps[0][:], w_q, over_pick[:, q, :],
                                                            start=(q == 0 and k == 0), stop=(q == WIN - 1 and k == 1))
                            last.then_inc(over_gathered, 1)
                            pe.reg_add(n_over, n_over, 1)

                        def fetch_leftovers(t, maxima):
                            g = t % NG
                            chunk = t // NG * WIN
                            snapped = lambda: chunk if isinstance(chunk, int) else pe.snap(chunk)

                            def first():
                                hold(pe, maxed, maxima, pe_passed)
                                fetch_leftover(snapped())

                            def more(left):
                                base = snapped()
                                with pe.Fori(4, left + 1) as rank:
                                    fetch_leftover(base)
                            leftovers(pe, bits_value(), top_count[0:1, bass.ds(g, 1)], first, more)
                            pe.reg_div(bits, bits, 2)

                        def bits_value():
                            return pe.snap(bits, min_val=0, max_val=2 * MORE * MORE)

                        def gather_rest(u, q):
                            n = WIN * u + q
                            for r in range(2):
                                pe.wait_ge(rest_pick_ready, 2 * n + r + 1)
                                if q == 0:
                                    wait(pe, rest_maxed, 2 * (u - 1) + r + 1)
                                for k in range(2):
                                    last = nc.tensor.matmul(rest_ps[r][:], weights(u, q, k), rest_pick[q % 2][r][:],
                                                            start=(q == 0 and k == 0), stop=(q == WIN - 1 and k == 1))
                                last.then_inc(rest_gathered, 1)

                        def later(fn, v, s, q, by):
                            k = WIN * s + q + by
                            if not (isinstance(v, int) and v == NV - 1 and k >= 2 * WIN):
                                fn(v + k // (2 * WIN), k // WIN % 2, k % WIN)

                        def pair(v, between):
                            for s in range(2):
                                for q in range(WIN):
                                    later(turn, v, s, q, 2)
                                    near(v, s, q, 0)
                                    later(make_code, v, s, q, 1)
                                    near(v, s, q, 1)
                                    make_rest_code(v, s, q)
                                    if q == 2 and leftover_beside(v):
                                        u = 2 * v + s
                                        fetch_leftovers(late(u), 2 * (WIN * u + q) + 1)
                                    if q > 0:
                                        gather_rest(2 * v + s, q - 1)
                                    elif s > 0 or not isinstance(v, int) or v > 0:
                                        gather_rest(2 * v + s - 1, WIN - 1)
                            if isinstance(v, int) and v == NV - 1:
                                gather_rest(NU - 1, WIN - 1)

                        def load(w):
                            hold(pe, stat, 9 * (w + 1), pe_passed)
                            pe.reg_mov(bits, pe.value_load(need[0:1, 0:1], min_val=0, max_val=MORE * MORE))

                        pe.wait_ge(ident_built, 1)
                        turn(0, 0, 0)
                        turn(0, 0, 1)
                        pe.wait_ge(rank_built, 3)
                        make_code(0, 0, 0)
                        walk(pe, pair, lambda w, s, q: None, load)
                        for g in range(NG - 2, NG):
                            fetch_leftovers(NG * (NG - 2) + g, 2 * STEPS)
                        load(NG - 1)
                        for g in range(NG):
                            fetch_leftovers(NG * (NG - 1) + g, 2 * STEPS)

                    @block.gpsimd
                    def _(pool):
                        def rest_of(v, s, q):
                            n = WIN * (2 * v + s) + q
                            wait(pool, rest_coded, n - WIN + 2)
                            hold(pool, code_ready, n + 1, pool_passed)
                            nc.gpsimd.tensor_scalar(rest[q][:], code[q % 2][:], DIAG + 2, None, ALU.is_ge
                                                    ).then_inc(rest_ready, 1)

                        def later(fn, v, s, q, by):
                            k = WIN * s + q + by
                            if not (isinstance(v, int) and v == NV - 1 and k >= 2 * WIN):
                                fn(v + k // (2 * WIN), k // WIN % 2, k % WIN)

                        def chunk_steps(c, seen):
                            c = bass.ds(c, 1)
                            flat = lambda t: t.rearrange("p o f -> p (o f)")

                            def link(ins, k):
                                ins.then_inc(norm, 1)
                                hold(pool, norm, seen + k, pool_passed)
                            x_c = flat(xs[:, c, :])
                            yield lambda: link(nc.gpsimd.tensor_tensor(hc[:], x_c, flat(mv[:, c, 0:1]).to_broadcast([P, F]), ALU.subtract), 1)
                            yield lambda: link(nc.gpsimd.tensor_tensor(hc[:], hc[:], rstd[:, c].to_broadcast([P, F]), ALU.mult), 2)
                            yield lambda: link(nc.gpsimd.tensor_scalar(hc[:], hc[:], 0.0, SCALE, ALU.max, ALU.mult), 3)
                            yield lambda: link(nc.gpsimd.tensor_copy(flat(hparts[:, c, 0, :]), hc[:]), 4)
                            yield lambda: nc.gpsimd.tensor_tensor(flat(hparts[:, c, 1, :]), hc[:], flat(hparts[:, c, 0, :]),
                                                                  ALU.subtract).then_inc(h_ready, 1)

                        def pair(v, between):
                            end = isinstance(v, int) and v > 0
                            steps = [] if end else list(chunk_steps(WIN + v, 4 * v))
                            for s in range(2):
                                for q in range(WIN):
                                    later(rest_of, v, s, q, 1)
                                    k = WIN * s + q
                                    if isinstance(v, int) and v == 0 and k == 0:
                                        pool.wait_ge(rstd_ready, 1)
                                    if k < len(steps):
                                        steps[k]()

                        nc.gpsimd.memset(ident[:], 0.0).then_inc(const_built, 1)
                        nc.gpsimd.memset(rank_w[:], 1.0).then_inc(const_built, 1)
                        pool.wait_ge(const_built, 2)
                        nc.gpsimd.affine_select(out=ident[:], in_=ident[:], compare_op=ALU.not_equal, fill=1.0,
                                                base=0, pattern=[[-1, P]], channel_multiplier=1).then_inc(const_built, 1)
                        nc.gpsimd.affine_select(out=rank_w[:], in_=rank_w[:], compare_op=ALU.is_gt, fill=0.0,
                                                base=0, pattern=[[1, P]], channel_multiplier=-1).then_inc(const_built, 1)
                        pool.wait_ge(const_built, 4)
                        nc.gpsimd.tensor_copy(ident16[:], ident[:]).then_inc(ident_built, 1)
                        nc.gpsimd.affine_select(out=rank_w[:], in_=rank_w[:], compare_op=ALU.not_equal, fill=DIAG,
                                                base=0, pattern=[[1, P]], channel_multiplier=-1).then_inc(rank_built, 1)
                        pool.wait_ge(rank_built, 1)
                        nc.gpsimd.tensor_copy(rank_rest[:], rank_w[:]).then_inc(rank_built, 1)
                        nc.gpsimd.tensor_scalar(count_rest[:], rank_w[:], -1.0, 1.0, ALU.mult, ALU.add).then_inc(rank_built, 1)
                        nc.gpsimd.memset(acc[:], 0.0).then_inc(acc_zero, 1)
                        nc.gpsimd.memset(a_diag[:], 0.0).then_inc(a_zero, 1)
                        rest_of(0, 0, 0)
                        pair(0, None)
                        with pool.Fori(1, NC - WIN) as v:
                            pair(v, None)
                        with pool.Fori(NC - WIN, NV - 1) as v:
                            for s in range(2):
                                for q in range(WIN):
                                    later(rest_of, v, s, q, 1)
                        pair(NV - 1, None)

                    @block.vector
                    def _(vec):
                        n_over = vec.alloc_register("vec_over")
                        vec.reg_mov(n_over, 0)
                        n_want = vec.alloc_register("vec_want")
                        vec.reg_mov(n_want, 0)
                        bits = vec.alloc_register("vec_bits")
                        vec.reg_mov(bits, 0)
                        vec.sem_inc(over_maxed, 1)
                        vec.sem_inc(slot_free, FREE)

                        def leftover_code(t):
                            slot = t % (2 * NG)
                            return rest_code[:, slot, :, :] if isinstance(slot, int) else \
                                rest_code[:, bass.ds(slot, 1), :, :].rearrange("p o q i -> p (o q) i")

                        def bits_value():
                            return vec.snap(bits, min_val=0, max_val=2 * MORE * MORE)

                        def pick_leftover(t):
                            def first():
                                nc.vector.tensor_scalar(over_pick[:], leftover_code(t), DIAG + 2, None, ALU.is_equal
                                                        ).then_inc(over_pick_ready, 1)
                            leftovers(vec, bits_value(), None, first, None)

                        def max_leftover(t):
                            before = vec.snap(n_over)
                            hold(vec, over_gathered, before + 1, vec_passed)
                            view = at(acc, t % NG, GW)
                            nc.vector.tensor_tensor(view, near_ps[0][:], view, ALU.max).then_inc(over_maxed, 1)
                            vec.reg_add(n_over, n_over, 1)

                        def max_leftovers(t):
                            def more(left):
                                nc.vector.memset(want[:], DIAG + 3).then_inc(want_set, 1)
                                vec.reg_add(n_want, n_want, 1)
                                with vec.Fori(4, left + 1) as rank:
                                    before = vec.snap(n_want)
                                    hold(vec, want_set, before, vec_passed)
                                    taken = vec.snap(n_over)
                                    hold(vec, over_maxed, taken + 1, vec_passed)
                                    nc.vector.tensor_scalar(over_pick[:], leftover_code(t), want[:, 0:1], None, ALU.is_equal
                                                            ).then_inc(over_pick_ready, 1)
                                    max_leftover(t)
                                    nc.vector.tensor_scalar(want[:], want[:], 1.0, None, ALU.add).then_inc(want_set, 1)
                                    vec.reg_add(n_want, n_want, 1)
                                before = vec.snap(n_want)
                                hold(vec, want_set, before, vec_passed)
                            g = t % NG
                            leftovers(vec, bits_value(), top_count[0:1, bass.ds(g, 1)], lambda: max_leftover(t), more)
                            vec.reg_div(bits, bits, 2)
                            vec.sem_inc(slot_free, 1)

                        def picks(v, s, q):
                            n = WIN * (2 * v + s) + q
                            vec.wait_ge(code_ready, n + 1)
                            for r in range(2):
                                nc.vector.tensor_scalar(pick[q % 2][r][:], code[q % 2][:], DIAG + r, None, ALU.is_equal
                                                        ).then_inc(pick_ready, 1)

                        def rest_picks(u, q):
                            n = WIN * u + q
                            wait(vec, rest_gathered, 2 * (n - 1))
                            vec.wait_ge(rest_code_ready, n + 1)
                            slot = u % (2 * NG)
                            src = rest_code[:, slot, q, :] if isinstance(slot, int) else \
                                rest_code[:, bass.ds(slot, 1), q, :].rearrange("p o i -> p (o i)")
                            for r in range(2):
                                nc.vector.tensor_scalar(rest_pick[q % 2][r][:], src, DIAG + r, None, ALU.is_equal
                                                        ).then_inc(rest_pick_ready, 1)

                        def near_max(u, q, r):
                            n = WIN * u + q
                            wait(vec, maxed, 2 * n + r)
                            vec.wait_ge(gathered, 2 * n + r + 1)
                            view = at(acc, u % NG, GW)
                            nc.vector.tensor_tensor(view, near_ps[r][:], view, ALU.max).then_inc(maxed, 1)

                        def rest_max(u, after):
                            view = at(acc, u % NG, GW)
                            for r in range(2):
                                wait(vec, rest_maxed, 2 * u + r)
                                if r == 0:
                                    vec.wait_ge(maxed, after)
                                vec.wait_ge(rest_gathered, 2 * WIN * (u + 1) - 1 + r)
                                nc.vector.tensor_tensor(view, rest_ps[r][:], view, ALU.max).then_inc(rest_maxed, 1)

                        def later(fn, v, s, q, by):
                            k = WIN * s + q + by
                            if not (isinstance(v, int) and v == NV - 1 and k >= 2 * WIN):
                                fn(v + k // (2 * WIN), k // WIN % 2, k % WIN)

                        def pair(v, between):
                            for s in range(2):
                                u = 2 * v + s
                                for q in range(WIN):
                                    between(s, WIN * q)
                                    begun = s > 0 or not isinstance(v, int) or v > 0
                                    if q == 1 and leftover_beside(v):
                                        pick_leftover(late(u))
                                    if q == 3 and leftover_beside(v):
                                        max_leftovers(late(u))
                                    if q > 0:
                                        rest_picks(u, q - 1)
                                    elif begun:
                                        rest_picks(u - 1, WIN - 1)
                                    if q == 1 and begun:
                                        rest_max(u - 1, 2 * WIN * u)
                                    between(s, WIN * q + 1)
                                    near_max(u, q, 0)
                                    between(s, WIN * q + 2)
                                    later(picks, v, s, q, 1)
                                    between(s, WIN * q + 3)
                                    near_max(u, q, 1)
                            if isinstance(v, int) and v == NV - 1:
                                rest_picks(NU - 1, WIN - 1)
                                rest_max(NU - 1, 2 * STEPS)

                        def count(w, s, place):
                            if s == 0:
                                return
                            k = {0: 0, 1: 1, 2: 2, 9: 3, 10: 4, 11: 5, 12: 6, 13: 7, 14: 8}.get(place)
                            if k is None:
                                return
                            if k == 0:
                                vec.wait_ge(last_in, 16 * NG * (w + 1))
                            else:
                                vec.wait_ge(stat, 9 * w + k)
                            if k == 0:
                                nc.vector.tensor_scalar(minus[:], last_row[:], DIAG, 1.0 - DIAG, ALU.is_ge, ALU.mult
                                                        ).then_inc(stat, 1)
                            elif k == 1:
                                nc.vector.tensor_tensor(minus[:], minus[:], last_row[:], ALU.add).then_inc(stat, 1)
                            elif k == 2:
                                nc.vector.tensor_reduce(rowmax[:], minus[:], AX.X, ALU.max).then_inc(stat, 1)
                            elif k == 3:
                                vec.wait_ge(maxrow_in, 16 * (w + 1))
                                nc.vector.tensor_reduce(top[:], maxrow[:].rearrange("o (g k) -> o g k", g=NG), AX.X, ALU.max
                                                        ).then_inc(stat, 1)
                            elif k == 4:
                                nc.vector.tensor_copy(top_count[:], top[:]).then_inc(stat, 1)
                            elif k < 7:
                                nc.vector.scalar_tensor_tensor(needy[:, k - 5, :], top[:], 3.0 + k - 5, bit[:, k - 5, :],
                                                               ALU.is_ge, ALU.mult).then_inc(stat, 1)
                            elif k == 7:
                                nc.vector.tensor_reduce(top[:, 0:1], needy[:].rearrange("o k g -> o (k g)"), AX.X, ALU.add
                                                        ).then_inc(stat, 1)
                            else:
                                nc.vector.tensor_copy(need[:], top[:, 0:1]).then_inc(stat, 1)

                        def load(w):
                            hold(vec, stat, 9 * (w + 1), vec_passed)
                            vec.reg_mov(bits, vec.value_load(need[0:1, 0:1], min_val=0, max_val=MORE * MORE))

                        link = linker(vec, norm_chain)
                        vec.wait_ge(x_in, 16)
                        window = range(0, WIN)
                        statistics(vec, link, window, var_ready, sqrt_done, 1)
                        link(nc.vector.tensor_tensor(h[:], xs[:, 0:WIN, :], mv[:, 0:WIN, 0:1].to_broadcast([P, WIN, F]),
                                                     ALU.subtract))
                        link(nc.vector.tensor_tensor(h[:], h[:], rstd[:, 0:WIN].unsqueeze(2).to_broadcast([P, WIN, F]),
                                                     ALU.mult))
                        link(nc.vector.tensor_scalar(h[:], h[:], 0.0, SCALE, ALU.max, ALU.mult))
                        link(nc.vector.tensor_copy(hparts[:, 0:WIN, 0, :], h[:]))
                        link(nc.vector.tensor_tensor(hparts[:, 0:WIN, 1, :], h[:], hparts[:, 0:WIN, 0, :], ALU.subtract))
                        vec.sem_inc(h_ready, WIN)
                        for g in range(2 * NG):
                            nc.vector.memset(bit[:, g // NG, g % NG:g % NG + 1], float(2 ** g)).then_inc(bit_set, 1)
                        vec.wait_ge(x_rest_in, 16)
                        statistics(vec, link, range(WIN, NC), var_ready, sqrt_done, 2)
                        vec.sem_inc(rstd_ready, 1)
                        vec.wait_ge(acc_zero, 1)
                        vec.wait_ge(bit_set, 2 * NG)
                        picks(0, 0, 0)
                        walk(vec, pair, lambda w, s, q: count(w, s, q), load)
                        for g in range(NG - 2, NG):
                            pick_leftover(NG * (NG - 2) + g)
                            max_leftovers(NG * (NG - 2) + g)
                        for place in range(WIN * WIN):
                            count(NG - 1, 1, place)
                        load(NG - 1)
                        for g in range(NG):
                            pick_leftover(NG * (NG - 1) + g)
                            max_leftovers(NG * (NG - 1) + g)
                        taken = vec.snap(n_over)
                        hold(vec, over_maxed, taken + 1, vec_passed)

        second = ExitStack()
        with second:
            wh = sb("wh", [P, NC, E], F32, second)
            h2t = acc
            gmax = sb("gmax", [P, 2 * H], F32, second)
            flag = sb("flag", [P, 1], I32, second)
            scope = ExitStack()
            with scope:
                h2 = sb("h2", [P, NC, F], F32, scope)
                mean_rstd = sb("mean_rstd", [P, NC], F32, scope)
                lmax = sb("lmax", [P, 2 * H], F32, scope)
                test = sb("test", [P, 3], F32, scope)
                spread = sb("spread", [P, H], F32, scope)
                x1_ps, x1_done, stats_ready, h2t_ps, h2t_done = (
                    sem("x1_ps"), sem("x1_done"), sem("stats_ready"), sem("h2t_ps"), sem("h2t_done"))
                h2_by_act, h2_by_vec = sem("h2_by_act"), sem("h2_by_vec")
                vec2, var2_ready, sqrt2_done, wh_ps, wh_by_vec, wh_by_act = (
                    sem("vec2"), sem("var2_ready"), sem("sqrt2_done"), sem("wh_ps"), sem("wh_by_vec"), sem("wh_by_act"))
                lmax_ready, gmax_ready = sem("lmax_ready"), sem("gmax_ready")
                wt_ps, wt_sb, wa_ps, wa_sb = sem("wt_ps"), sem("wt_sb"), sem("wa_ps"), sem("wa_sb")
                NW = NC // 2
                WV = 10
                HB = NC // 2
                HG = NG // 2
                with nc.Block() as block:
                    @block.tensor
                    def _(pe):
                        for g in range(NG):
                            if g >= 4:
                                pe.wait_ge(x1_done, g - 3)
                            for k in range(GB):
                                b = GB * g + k
                                last = nc.tensor.transpose(banks[g % 4][:, k * P:(k + 1) * P], acc[:, b * P:(b + 1) * P],
                                                           ident[:])
                            last.then_inc(x1_ps, 1)
                            if g == 3:
                                pe.wait_ge(w_in, 16)
                                nc.tensor.transpose(banks[4][:, 0:P], w_ext[:, 0:F], ident[:]).then_inc(wt_ps, 1)
                        pe.wait_ge(wt_sb, 1)
                        pe.wait_ge(a_in, 16 * 2 * H)
                        nc.tensor.matmul(banks[5][:, 0:2 * H], wt[:], a_diag[:], start=True, stop=True).then_inc(wa_ps, 1)
                        pe.wait_ge(x1_done, NG)
                        pe.wait_ge(wa_sb, 1)
                        def turn_h2(g):
                            if g < HG:
                                pe.wait_ge(h2_by_act, GB * (g + 1))
                            else:
                                pe.wait_ge(h2_by_vec, GB * (g + 1 - HG))
                            if g >= 4:
                                pe.wait_ge(h2t_done, g - 3)
                            for k in range(GB):
                                last = nc.tensor.transpose(banks[4 + g % 4][:, k * P:(k + 1) * P],
                                                           h2[:, GB * g + k, :], ident[:])
                            last.then_inc(h2t_ps, 1)

                        def make_wh(w):
                            pe.wait_ge(h2t_done, (2 * w) // GB + 1)
                            if w >= 4:
                                if w - 4 < WV:
                                    pe.wait_ge(wh_by_vec, w - 3)
                                else:
                                    pe.wait_ge(wh_by_act, w - 3 - WV)
                            for k in range(2):
                                c = 2 * w + k
                                last = nc.tensor.matmul(banks[w % 4][:, k * E:(k + 1) * E], h2t[:, c * P:(c + 1) * P],
                                                        w_ext[:], start=True, stop=True)
                            last.then_inc(wh_ps, 1)
                        for g in range(HG):
                            turn_h2(g)
                        for g in range(HG, NG):
                            turn_h2(g)
                            for w in range(2 * (g - HG), 2 * (g - HG) + 2):
                                make_wh(w)
                        for w in range(NW // 2, NW):
                            make_wh(w)

                    def copy_wh(engine_copy, w):
                        return engine_copy(wh[:, 2 * w:2 * w + 2, :],
                                           banks[w % 4][:, 0:2 * E].rearrange("p (k e) -> p k e", e=E))

                    @block.vector
                    def _(vec):
                        link = linker(vec, vec2)
                        for half in range(2):
                            r = slice(half * HB, (half + 1) * HB)
                            for g in range(half * HG, (half + 1) * HG + 1):
                                if g < (half + 1) * HG:
                                    vec.wait_ge(x1_ps, g + 1)
                                    view = xs[:, GB * g:GB * (g + 1), :]
                                    nc.vector.scalar_tensor_tensor(view, banks[g % 4][:].rearrange("p (b f) -> p b f", f=F),
                                                                   1.0 / SCALE, view, ALU.mult, ALU.add).then_inc(x1_done, 1)
                                if g > half * HG:
                                    vec.wait_ge(x1_done, g)
                                    for b in range(GB * (g - 1), GB * g):
                                        nc.vector.bn_stats(stats[:, b, :], xs[:, b, :]).then_inc(stats_ready, 1)
                            for b in range(half * HB, (half + 1) * HB):
                                vec.wait_ge(stats_ready, b + 1)
                                last = nc.vector.bn_aggr(mv[:, b, :], stats[:, b, :])
                            link(last)
                            nc.vector.tensor_scalar(rstd[:, r], mv[:, r, 1], EPS, None, ALU.add).then_inc(var2_ready, 1)
                            link(nc.vector.tensor_scalar(vareps[:, r], mv[:, r, 1], EPS, -0.5, ALU.add, ALU.mult))
                            vec.wait_ge(sqrt2_done, half + 1)
                            link(nc.vector.reciprocal(rstd[:, r], rstd[:, r]))
                            link(nc.vector.tensor_tensor(vareps[:, r], vareps[:, r], rstd[:, r], ALU.mult))
                            link(nc.vector.tensor_tensor(vareps[:, r], vareps[:, r], rstd[:, r], ALU.mult))
                            link(nc.vector.scalar_tensor_tensor(rstd[:, r], vareps[:, r], 1.5, rstd[:, r], ALU.add, ALU.mult))
                            if half == 0:
                                nc.vector.scalar_tensor_tensor(mean_rstd[:, r], mv[:, r, 0], -1.0, rstd[:, r],
                                                               ALU.mult, ALU.mult).then_inc(var2_ready, 1)
                        for b in range(HB, NC):
                            nc.vector.tensor_scalar(h2[:, b, :], xs[:, b, :], mv[:, b, 0:1], rstd[:, b:b + 1],
                                                    ALU.subtract, ALU.mult).then_inc(h2_by_vec, 1)
                        for w in range(WV):
                            vec.wait_ge(wh_ps, w + 1)
                            copy_wh(nc.vector.tensor_copy, w).then_inc(wh_by_vec, 1)
                        vec.wait_ge(wh_by_vec, WV)
                        vec.wait_ge(wh_by_act, NW - WV)
                        dst = wh[:, :, F + H:E].rearrange("p c h -> p h c")
                        link(nc.vector.tensor_reduce(lmax[:, 0:H], dst, AX.X, ALU.max))
                        link(nc.vector.tensor_reduce(lmax[:, H:2 * H], dst, AX.X, ALU.min, negate=True))
                        vec.sem_inc(lmax_ready, 1)
                        vec.wait_ge(gmax_ready, 1)
                        link(nc.vector.tensor_tensor(spread[:], gmax[:, 0:H], gmax[:, H:2 * H], ALU.add))
                        link(nc.vector.tensor_reduce(test[:, 0:1], spread[:], AX.X, ALU.max))
                        link(nc.vector.tensor_reduce(test[:, 1:2], gmax[:], AX.X, ALU.max))
                        link(nc.vector.tensor_scalar(test[:, 0:1], test[:, 0:1], SPREAD, None, ALU.is_le))
                        link(nc.vector.tensor_scalar(test[:, 1:2], test[:, 1:2], LARGEST, None, ALU.is_le))
                        link(nc.vector.tensor_tensor(flag[:], test[:, 0:1], test[:, 1:2], ALU.mult))

                    @block.scalar
                    def _(act):
                        act.wait_ge(wt_ps, 1)
                        nc.scalar.copy(wt[:], banks[4][:, 0:P]).then_inc(wt_sb, 1)

                        def sqrt(half):
                            r = slice(half * HB, (half + 1) * HB)
                            act.wait_ge(var2_ready, 2 * half + 1)
                            nc.scalar.activation(rstd[:, r], rstd[:, r], ACT.Sqrt).then_inc(sqrt2_done, 1)
                        sqrt(0)
                        act.wait_ge(wa_ps, 1)
                        nc.scalar.copy(w_ext[:, F:E], banks[5][:, 0:2 * H]).then_inc(wa_sb, 1)
                        act.wait_ge(var2_ready, 2)

                        def normalise(g):
                            for b in range(GB * g, GB * (g + 1)):
                                nc.scalar.activation(h2[:, b, :], xs[:, b, :], ACT.Relu, bias=mean_rstd[:, b:b + 1],
                                                     scale=rstd[:, b:b + 1]).then_inc(h2_by_act, 1)

                        def turned_group(g):
                            act.wait_ge(h2t_ps, g + 1)
                            nc.scalar.activation(h2t[:, g * GW:(g + 1) * GW], banks[4 + g % 4][:], ACT.Relu
                                                 ).then_inc(h2t_done, 1)
                        for g in range(HG):
                            normalise(g)
                            if g == 2:
                                sqrt(1)
                            if g > 0:
                                turned_group(g - 1)
                        for g in range(HG - 1, NG):
                            turned_group(g)
                        for w in range(WV, NW):
                            act.wait_ge(wh_ps, w + 1)
                            copy_wh(nc.scalar.copy, w).then_inc(wh_by_act, 1)

                    @block.gpsimd
                    def _(pool):
                        pool.wait_ge(lmax_ready, 1)
                        nc.gpsimd.partition_all_reduce(gmax[:], lmax[:], P, bass.bass_isa.ReduceOp.max).then_inc(gmax_ready, 1)

            narrow = nc.values_load(flag[0:1, 0:1], min_val=0, max_val=1)
            v = dict(locals())
            with nc.If(narrow == 1):
                factored_attention(nc, sem, sb, banks, v)
            with nc.Else():
                general_attention(nc, sem, sb, banks, v)


def factored_attention(nc, sem, sb, banks, v):
    N, F, H, D, NC, NG, GW, GB, E = (v[k] for k in ("N", "F", "H", "D", "NC", "NG", "GW", "GB", "E"))
    wh, h2t, xs, w_ext, gmax = v["wh"], v["h2t"], v["xs"], v["w_ext"], v["gmax"]
    mask_dram, out_dram = v["mask_dram"], v["out_dram"]
    NP = H // 2
    C1 = D + 1
    C3 = 3 * C1
    CG = 2 * C3
    CM = 2 * C3 + 2
    CV = 4 * C3 + 2
    OB = (0, 3 * C3 + 2)
    OD = (C3, 2 * C3 + 2)
    OG = (0, 2 * C3 + 2)
    PIECE = 8
    NPC = NC // PIECE
    NGB = 8
    BIG = float(2 ** 30)
    out_view = out_dram.rearrange("(b p) f -> p b f", p=P)
    mask_view = mask_dram.rearrange("(c p) i -> p c i", p=P)
    scope = ExitStack()
    with scope:
        vals = sb("vals", [P, NC * NP, CV], BF16, scope)
        ndcol = sb("ndcol", [P, NC, H], F32, scope)
        dbig = sb("dbig", [P, NC, H], F32, scope)
        amul = sb("amul", [P, NC, H], F32, scope)
        cmul = sb("cmul", [P, NC, H], F32, scope)
        mean = sb("mean", [P, F], F32, scope)
        mask = sb("mask", [P, NC, GW], BF16, scope)
        srow = sb("srow", [P, H, GW], F32, scope)
        mask_in = [sem(f"mask_in{i}") for i in range(NPC)]
        srow_in = [sem(f"srow_in{a}") for a in range(NP)]
        s_dram = v["s_dram"]

        def load(sp, g, p):
            sp.dma_start(mask[:, p * PIECE:(p + 1) * PIECE, :],
                         mask_view[:, p * PIECE:(p + 1) * PIECE, bass.ts(g, GW)]).then_inc(mask_in[p], 16)

        def rows(sp, g, a):
            sp.dma_start(srow[:, 2 * a:2 * a + 2, :],
                         s_dram[2 * a:2 * a + 2, bass.ts(g, GW)].partition_broadcast(P)).then_inc(srow_in[a], 16)


        prep = ExitStack()
        with prep:
            part = [sb(f"part{i}", [P, NC * NP, 2, C1], F32, prep) for i in range(2)]
            bexp = sb("bexp", [P, NC, H], F32, prep)
            dexp = sb("dexp", [P, NC, H], F32, prep)
            z0 = sb("z0", [P, NC, H], F32, prep)
            z5 = sb("z5", [P, NC, H], F32, prep)
            zm = sb("zm", [P, NC, H], F32, prep)
            ones = sb("ones", [P, P], F32, prep)
            vec5, exp_in, exp_out, ones_ready, mean_ps, mean_done = (sem(n) for n in ("vec5", "exp_in", "exp_out",
                                                                     "ones_ready", "mean_ps", "mean_done"))
            ones_col, s_ps, s_sb, s_out = sem("ones_col"), sem("s_ps"), sem("s_sb"), sem("s_out")
            full, full_by_pool, high_done, second_ready, mid_done = (
                sem(n) for n in ("full", "full_by_pool", "high_done", "second_ready", "mid_done"))
            s_rows = h2t[0:H, :]
            NQ = 4
            QC = NC // NQ
            offsets = (OB, OD)
            exps = (bexp, dexp)
            heads = [part[i][:].rearrange("p (c a) k e -> p c (a k) e", c=NC) for i in range(2)]
            wh_heads = wh[:, :, 0:F].rearrange("p c (h e) -> p c h e", h=H)

            def scaled(engine, i, q):
                r = slice(q * QC, (q + 1) * QC)
                return engine.tensor_tensor(heads[i][:, r, :, 0:D], wh_heads[:, r],
                                            exps[i][:, r].unsqueeze(3).to_broadcast([P, QC, H, D]), ALU.mult)

            def weight(engine, i, q):
                r = slice(q * QC, (q + 1) * QC)
                return engine.tensor_copy(heads[i][:, r, :, D:C1], exps[i][:, r].unsqueeze(3))

            def piece(i, q, k, n):
                r = slice(q * QC * NP, (q + 1) * QC * NP)
                off = offsets[i][k] + n * C1
                return part[i][:, r, k, :], vals[:, r, off:off + C1]

            with nc.Block() as block:
                @block.sync
                def _(sp):
                    for p in range(NPC):
                        load(sp, 0, p)
                    sp.wait_ge(s_sb, NG)
                    sp.dma_start(s_dram, s_rows).then_inc(s_out, 16)
                    sp.wait_ge(s_out, 16)
                    for a in range(NP):
                        rows(sp, 0, a)

                @block.tensor
                def _(pe):
                    for g in range(NG):
                        if g >= 4:
                            pe.wait_ge(s_sb, g - 3)
                        nc.tensor.matmul(banks[4 + g % 4][0:H, :], w_ext[:, F:F + H], h2t[:, g * GW:(g + 1) * GW],
                                         start=True, stop=True).then_inc(s_ps, 1)
                    pe.wait_ge(ones_ready, 1)
                    for c in range(NC):
                        last = nc.tensor.matmul(banks[0][:, 0:F], ones[:], wh[:, c, 0:F], start=(c == 0), stop=(c == NC - 1))
                    last.then_inc(mean_ps, 1)

                @block.gpsimd
                def _(pool):
                    nc.gpsimd.memset(ones[:], 1.0).then_inc(ones_ready, 1)
                    nc.gpsimd.memset(vals[:, :, OD[0] + C3:OD[0] + C3 + 1], 1.0).then_inc(ones_col, 1)
                    nc.gpsimd.memset(vals[:, :, OD[0] + C3 + 1:OD[0] + C3 + 2], 0.0).then_inc(ones_col, 1)
                    pool.wait_ge(exp_out, 2)
                    for q in range(NQ):
                        scaled(nc.gpsimd, 1, q).then_inc(full_by_pool, 1)
                        weight(nc.gpsimd, 1, q).then_inc(full_by_pool, 1)
                    pool.wait_ge(ones_col, 2)

                @block.scalar
                def _(act):
                    for n, t in enumerate((bexp, dexp)):
                        act.wait_ge(exp_in, n + 1)
                        nc.scalar.activation(t[:], t[:], ACT.Exp).then_inc(exp_out, 1)

                    for g in range(NG):
                        act.wait_ge(s_ps, g + 1)
                        nc.scalar.copy(s_rows[:, g * GW:(g + 1) * GW], banks[4 + g % 4][0:H, :]).then_inc(s_sb, 1)

                    def high(i, q):
                        if i == 0:
                            act.wait_ge(full, 2 * (q + 1))
                        else:
                            act.wait_ge(full_by_pool, 2 * (q + 1))
                        for k in range(2):
                            src, dst = piece(i, q, k, 0)
                            nc.scalar.copy(dst, src).then_inc(high_done, 1)

                    def middle(i, q, n):
                        for k in range(2):
                            act.wait_ge(second_ready, 2 * n + k + 1)
                            src, dst = piece(i, q, k, 1)
                            nc.scalar.copy(dst, src).then_inc(mid_done, 1)

                    order = [(0, q) for q in range(NQ)] + [(1, q) for q in range(NQ)]
                    for n in range(2 * NQ + 1):
                        if n < 2 * NQ:
                            high(*order[n])
                        if n > 0:
                            middle(*order[n - 1], n - 1)
                        if n == 3:
                            act.wait_ge(mean_ps, 1)
                            nc.scalar.mul(mean[:], banks[0][:, 0:F], 1.0 / N).then_inc(mean_done, 1)
                        if n == 4:
                            for m, t in enumerate((amul, cmul)):
                                act.wait_ge(exp_in, m + 3)
                                nc.scalar.activation(t[:], t[:], ACT.Exp).then_inc(exp_out, 1)

                @block.vector
                def _(vec):
                    count = [0]

                    def link(ins):
                        count[0] += 1
                        ins.then_inc(vec5, 1)
                        vec.wait_ge(vec5, count[0])

                    dmax = gmax[:, 0:H].unsqueeze(1).to_broadcast([P, NC, H])
                    link(nc.vector.tensor_tensor(bexp[:], wh[:, :, F + H:E], dmax, ALU.subtract))
                    link(nc.vector.tensor_scalar(dexp[:], bexp[:], ALPHA, None, ALU.mult))
                    vec.sem_inc(exp_in, 2)
                    nc.vector.tensor_scalar(ndcol[:], wh[:, :, F + H:E], -1.0, None, ALU.mult)
                    nc.vector.tensor_scalar(dbig[:], wh[:, :, F + H:E], BIG, None, ALU.mult)
                    link(nc.vector.tensor_tensor(z0[:], wh[:, :, F:F + H], dmax, ALU.add))
                    link(nc.vector.tensor_scalar(z5[:], z0[:], ALPHA, None, ALU.mult))
                    vec.wait_ge(exp_out, 1)
                    for q in range(NQ):
                        scaled(nc.vector, 0, q).then_inc(full, 1)
                        weight(nc.vector, 0, q).then_inc(full, 1)
                    link(nc.vector.tensor_tensor(zm[:], z0[:], z5[:], ALU.max))
                    link(nc.vector.tensor_tensor(amul[:], z0[:], zm[:], ALU.subtract))
                    link(nc.vector.tensor_tensor(cmul[:], z5[:], zm[:], ALU.subtract))
                    vec.sem_inc(exp_in, 2)

                    def second(i, q, n):
                        for k in range(2):
                            vec.wait_ge(high_done, 2 * n + k + 1)
                            src, dst = piece(i, q, k, 0)
                            nc.vector.tensor_tensor(src, src, dst, ALU.subtract).then_inc(second_ready, 1)

                    def third(i, q, n):
                        for k in range(2):
                            vec.wait_ge(mid_done, 2 * n + k + 1)
                            src, dst = piece(i, q, k, 1)
                            last = nc.vector.tensor_tensor(piece(i, q, k, 2)[1], src, dst, ALU.subtract)
                        return last
                    order = [(0, q) for q in range(NQ)] + [(1, q) for q in range(NQ)]
                    for n in range(2 * NQ + 1):
                        if n < 2 * NQ:
                            second(*order[n], n)
                        if n > 0:
                            last = third(*order[n - 1], n - 1)
                    link(last)
                    vec.wait_ge(exp_out, 4)
                    vec.wait_ge(mean_done, 1)

        step = [sb(f"step{i}", [P, GW], BF16, scope) for i in range(8)]
        hmat = [sb(f"hmat{i}", [P, GW], BF16, scope) for i in range(NGB)]
        own = sb("own", [P, GB, 2 * CG], F32, scope)
        all_ = sb("all", [P, GB, CM], F32, scope)
        bsum = sb("bsum", [P, GB, 2, C1], F32, scope)
        dsum = sb("dsum", [P, GB, 2, C3], F32, scope)
        inv = sb("inv", [P, GB, 2], F32, scope)
        empty = sb("empty", [P, GB], F32, scope)
        o = sb("o2", [P, GB, F], F32, scope)
        neg = sb("neg2", [P, GB, F], F32, scope)

        piece_free = [sem(f"piece_free{i}") for i in range(NPC - 1)]
        step_ready = sem("step_ready")
        hmat_ready, hmat_free = sem("hmat_ready"), sem("hmat_free")
        swept, fin_free = sem("swept"), sem("fin_free")
        cleared = [sem("cleared_by_act"), sem("cleared_by_vec")]
        den_ready, inv_ready, chain = sem("den_ready"), sem("inv_ready"), sem("chain")
        neg_ready, neg_exp, o_ready, o_out = sem("neg_ready"), sem("neg_exp"), sem("o_ready2"), sem("o_out")
        spass, apass, ppass, vpass = sem("spass"), sem("apass"), sem("ppass"), sem("vpass")
        last_sums = sem("last_sums")
        U = 2 * NC

        def by_group(t, g):
            return t[:, g * GB:(g + 1) * GB, :] if isinstance(g, int) else t[:, bass.ts(g, GB), :]

        def sums(ops, link, g, a):
            for k in range(2):
                h = 2 * a + k
                ob = OB[k] if k == 0 else OB[k] - 2
                od = OD[k] if k == 0 else OD[k] - 2
                md = k * (C3 + 2)
                bs, ds = bsum[:, :, k, :], dsum[:, :, k, :]
                sum_d = ds[:, :, 0:C1]
                link(ops.tensor_tensor(bs, own[:, :, ob + 2 * C1:ob + C3], own[:, :, ob + C1:ob + 2 * C1], ALU.add))
                link(ops.tensor_tensor(bs, bs, own[:, :, ob:ob + C1], ALU.add))
                link(ops.tensor_tensor(ds, all_[:, :, md:md + C3], own[:, :, od:od + C3], ALU.subtract))
                link(ops.tensor_tensor(sum_d, sum_d, ds[:, :, C1:2 * C1], ALU.add))
                link(ops.tensor_tensor(sum_d, sum_d, ds[:, :, 2 * C1:C3], ALU.add))
                link(ops.tensor_tensor(bs, bs, by_group(amul, g)[:, :, h:h + 1].to_broadcast([P, GB, C1]), ALU.mult))
                link(ops.tensor_tensor(sum_d, sum_d, by_group(cmul, g)[:, :, h:h + 1].to_broadcast([P, GB, C1]), ALU.mult))
                link(ops.tensor_tensor(bs, bs, sum_d, ALU.add))
            link(ops.tensor_scalar(empty[:], all_[:, :, C3], 0.0, None, ALU.is_equal))
            for k in range(2):
                h = 2 * a + k
                link(ops.tensor_tensor(bsum[:, :, k, D], bsum[:, :, k, D], empty[:], ALU.add))
                link(ops.tensor_tensor(dsum[:, :, k, 0:D], empty[:].unsqueeze(2).to_broadcast([P, GB, D]),
                                       mean[:, h * D:(h + 1) * D].unsqueeze(1).to_broadcast([P, GB, D]), ALU.mult))
                link(ops.tensor_tensor(bsum[:, :, k, 0:D], bsum[:, :, k, 0:D], dsum[:, :, k, 0:D], ALU.add))

        def quotients(ops, link, a):
            for k in range(2):
                h = 2 * a + k
                link(ops.tensor_tensor(o[:, :, h * D:(h + 1) * D], bsum[:, :, k, 0:D],
                                       inv[:, :, k:k + 1].to_broadcast([P, GB, D]), ALU.mult))

        def elu_parts(ops, engine, link, g):
            link(ops.tensor_scalar(neg[:], o[:], 0.0, None, ALU.min))
            engine.sem_inc(neg_ready, 1)
            link(ops.tensor_scalar(o[:], o[:], 0.0, -1.0, ALU.max, ALU.add))
            link(ops.tensor_tensor(o[:], o[:], by_group(xs, g), ALU.add))

        LSUM = 2 * 8 + 1 + 2 * 3
        LPG = 2 * (LSUM + 2) + 4

        by_act = [(c, k) for c in range(NC) for k in range(2) if k == 1 or c % 2 == 1]
        NS = len(by_act)
        assert NS % len(step) == 0

        def clear_banks(copy, i):
            for b in range(i, GB, 2):
                copy(own[:, b, :], banks[b][:, 0:2 * CG]).then_inc(cleared[i], 1)
            copy(all_[:, 2 * i:2 * i + 2, :], banks[4 + i][:, 0:2 * CM].rearrange("p (b e) -> p b e", e=CM)
                 ).then_inc(cleared[i], 1)

        with nc.Block() as block:
            @block.sync
            def _(sp):
                with sp.Fori(1, NG) as g:
                    hold(sp, hmat_ready, U * (2 * g - 1), spass)
                    rows(sp, g, 0)
                    for p in range(NPC - 1):
                        hold(sp, piece_free[p], g, spass)
                        load(sp, g, p)
                    hold(sp, hmat_ready, U * 2 * g, spass)
                    rows(sp, g, 1)
                    hold(sp, swept, NP * g, spass)
                    load(sp, g, NPC - 1)
                    sp.wait_ge(o_ready, g)
                    sp.dma_start(out_view[:, bass.ts(g - 1, GB), :], o[:]).then_inc(o_out, 16)
                sp.wait_ge(o_ready, NG)
                sp.dma_start(out_view[:, (NG - 1) * GB:NG * GB, :], o[:]).then_inc(o_out, 16)
                sp.wait_ge(o_out, 16 * NG)

            @block.tensor
            def _(pe):
                def sweep(g, a, s):
                    for c in range(NC):
                        for k in range(2):
                            pe.wait_ge(hmat_ready, U * s + 2 * c + k + 1)
                            m = hmat[(2 * c + k) % NGB]
                            for b in range(GB):
                                if c == 0 and k == 0:
                                    pe.wait_ge(cleared[b % 2], 3 * s + b // 2 + 1)
                                last = nc.tensor.matmul(banks[b][:, k * CG:(k + 1) * CG], m[:, b * P:(b + 1) * P],
                                                        vals[:, NP * c + a, OG[k]:OG[k] + CG], start=(c == 0 and k == 0),
                                                        stop=(c == NC - 1), skip_group_check=True)
                            last.then_inc(hmat_free, 1)
                        for b in range(GB):
                            if c == 0 and b % 2 == 0:
                                pe.wait_ge(cleared[b // 2], 3 * s + 3)
                            last = nc.tensor.matmul(banks[4 + b // 2][:, b % 2 * CM:(b % 2 + 1) * CM],
                                                    mask[:, c, b * P:(b + 1) * P], vals[:, NP * c + a, OD[0]:OD[0] + CM],
                                                    start=(c == 0 and b % 2 == 0), stop=(c == NC - 1), skip_group_check=True)
                        if c == NC - 1:
                            last.then_inc(swept, 1)
                        elif a == NP - 1 and c % PIECE == PIECE - 1:
                            last.then_inc(piece_free[c // PIECE], 1)
                with pe.Fori(0, NG) as g:
                    sweep(g, 0, 2 * g)
                    sweep(g, 1, 2 * g + 1)

            @block.scalar
            def _(act):
                act.sem_inc(cleared[0], 3)

                def steps(g, s, a, n, first):
                    c, k = by_act[n]
                    if n == 0:
                        act.wait_ge(srow_in[a], 16 * (g + 1))
                    if not first or n >= len(step):
                        before_c, before_k = by_act[n - len(step)]
                        act.wait_ge(hmat_ready, U * s + 2 * before_c + before_k + 1 - (U if n < len(step) else 0))
                    nc.scalar.activation(step[n % len(step)][:], srow[:, 2 * a + k, :], ACT.Relu,
                                         bias=dbig[:, c, 2 * a + k:2 * a + k + 1], scale=BIG).then_inc(step_ready, 1)

                def clear(s):
                    act.wait_ge(fin_free, s + 1)
                    hold(act, swept, s + 1, apass)
                    clear_banks(nc.scalar.copy, 0)

                def sweep(g, a, s, first=False):
                    for n in range(NS):
                        if n == len(step) - 1 and not first:
                            clear(s - 1)
                        steps(g, s, a, n, first)

                def elu(g):
                    act.wait_ge(neg_ready, g + 1)
                    nc.scalar.activation(neg[:], neg[:], ACT.Exp).then_inc(neg_exp, 1)

                sweep(0, 0, 0, True)
                sweep(0, 1, 1)
                with act.Fori(1, NG) as g:
                    sweep(g, 0, 2 * g)
                    elu(g - 1)
                    sweep(g, 1, 2 * g + 1)
                clear(2 * NG - 1)
                elu(NG - 1)

            @block.vector
            def _(vec):
                def sweep(g, a, s, first=False):
                    vec.wait_ge(srow_in[a], 16 * (g + 1))
                    for c in range(NC):
                        if a == 0 and c % PIECE == 0:
                            vec.wait_ge(mask_in[c // PIECE], 16 * (g + 1))
                        for k in range(2):
                            n = U * s + 2 * c + k
                            if not first or 2 * c + k >= NGB:
                                vec.wait_ge(hmat_free, n + 1 - NGB)
                            m = hmat[(2 * c + k) % NGB]
                            if (c, k) in by_act:
                                n_step = by_act.index((c, k))
                                vec.wait_ge(step_ready, NS * s + n_step + 1)
                                nc.vector.tensor_tensor(m[:], step[n_step % len(step)][:], mask[:, c, :], ALU.min).then_inc(hmat_ready, 1)
                            else:
                                nc.vector.scalar_tensor_tensor(m[:], srow[:, 2 * a + k, :], ndcol[:, c, 2 * a + k:2 * a + k + 1],
                                                               mask[:, c, :], ALU.is_gt, ALU.mult).then_inc(hmat_ready, 1)
                        if c == 2 and not first:
                            clear(s - 1)
                        if c == 22 and not first:
                            invert(s - 1)

                def clear(s):
                    vec.wait_ge(fin_free, s + 1)
                    hold(vec, swept, s + 1, vpass)
                    clear_banks(nc.vector.tensor_copy, 1)

                def invert(s):
                    vec.wait_ge(den_ready, s + 1)
                    nc.vector.reciprocal(inv[:], bsum[:, :, :, D]).then_inc(inv_ready, 1)

                vec.sem_inc(cleared[1], 3)
                sweep(0, 0, 0, True)
                sweep(0, 1, 1)
                with vec.Fori(1, NG) as g:
                    sweep(g, 0, 2 * g)
                    sweep(g, 1, 2 * g + 1)

                count = [0]

                def link(ins):
                    count[0] += 1
                    ins.then_inc(last_sums, 1)
                    vec.wait_ge(last_sums, count[0])
                vec.wait_ge(chain, LPG * (NG - 1) + LSUM + 2)
                clear(2 * NG - 1)
                for i in range(2):
                    vec.wait_ge(cleared[i], 3 * (2 * NG + 1))
                sums(nc.vector, link, NG - 1, NP - 1)
                link(nc.vector.reciprocal(inv[:], bsum[:, :, :, D]))
                quotients(nc.vector, link, NP - 1)
                elu_parts(nc.vector, vec, link, NG - 1)
                vec.wait_ge(neg_exp, NG)
                link(nc.vector.tensor_tensor(o[:], o[:], neg[:], ALU.add))
                vec.sem_inc(o_ready, 1)

            @block.gpsimd
            def _(pool):
                pool.sem_inc(fin_free, 1)
                total = [0]

                def linked(base, static):
                    def link(ins):
                        total[0] += 1
                        ins.then_inc(chain, 1)
                        wait(chain, base + total[0], static)
                    return link

                def wait(semaphore, value, static):
                    pool.wait_ge(semaphore, value) if static else hold(pool, semaphore, value, ppass)

                def finish(g, a, s, base, static):
                    link = linked(base, static)
                    for i in range(2):
                        wait(cleared[i], 3 * (s + 2), static)
                    sums(nc.gpsimd, link, g, a)
                    pool.sem_inc(den_ready, 1)
                    pool.sem_inc(fin_free, 1)
                    wait(inv_ready, s + 1, static)
                    quotients(nc.gpsimd, link, a)

                def output(g, base, static):
                    link = linked(base, static)
                    elu_parts(nc.gpsimd, pool, link, g)
                    wait(neg_exp, g + 1, static)
                    link(nc.gpsimd.tensor_tensor(o[:], o[:], neg[:], ALU.add))
                    pool.sem_inc(o_ready, 1)

                finish(0, 0, 0, 0, True)
                finish(0, 1, 1, 0, True)
                output(0, 0, True)
                assert total[0] == LPG
                with pool.Fori(1, NG - 1) as g:
                    total[0] = 0
                    hold(pool, o_out, 16 * g, ppass)
                    finish(g, 0, 2 * g, LPG * g, False)
                    finish(g, 1, 2 * g + 1, LPG * g, False)
                    output(g, LPG * g, False)
                total[0] = 0
                pool.wait_ge(o_out, 16 * (NG - 1))
                finish(NG - 1, 0, 2 * (NG - 1), LPG * (NG - 1), True)


def general_attention(nc, sem, sb, banks, v):
    N, F, H, D, NC, NG, GW, GB, E = (v[k] for k in ("N", "F", "H", "D", "NC", "NG", "GW", "GB", "E"))
    wh, h2t, xs, ident, w_ext = v["wh"], v["h2t"], v["xs"], v["ident"], v["w_ext"]
    adj_rows, out_rows = v["adj_rows"], v["out_rows"]
    scope = ExitStack()
    with scope:
        wrep = sb("wrep", [P, H, P], F32, scope)
        drow = sb("drow", [P, H, N], F32, scope)
        arow = sb("arow", [P, N], I32, scope)
        keep = sb("keep", [P, N], F32, scope)
        fill = sb("fill", [P, N], F32, scope)
        e = sb("e", [P, N], F32, scope)
        pt = arow[:].bitcast(F32)
        ssrc = sb("ssrc", [P, H], F32, scope)
        nmax = sb("nmax", [P, 1], F32, scope)
        den = sb("den", [P, H], F32, scope)
        rden = sb("rden", [P, 1], F32, scope)
        o = sb("o", [P, F], F32, scope)
        neg = sb("neg", [P, F], F32, scope)
        wrep_ready, drow_ps, drow_done = sem("wrep_ready"), sem("drow_ps"), sem("drow_done")
        arow_in, arow_free, e_ready, p_ready, p_ps, p_evac, pv, vec3, s_elu, elu_exp, o_ready, stored = (
            sem(n) for n in ("arow_in", "arow_free", "e_ready", "p_ready", "p_ps", "p_evac", "pv", "vec3", "s_elu",
                             "elu_exp", "o_ready", "stored"))
        VL = 3 + 6 * H + 3
        with nc.Block() as block:
            @block.sync
            def _(sp):
                with sp.Fori(0, NC) as b:
                    sp.wait_ge(arow_free, b + 1)
                    sp.dma_start(arow[:], adj_rows[b]).then_inc(arow_in, 16)
                    sp.wait_ge(o_ready, b + 1)
                    sp.dma_start(out_rows[b], o[:]).then_inc(stored, 16)
                sp.wait_ge(stored, 16 * NC)

            @block.tensor
            def _(pe):
                pe.wait_ge(wrep_ready, 1)
                for h in range(H):
                    for g in range(NG):
                        n = NG * h + g
                        if n >= 4:
                            pe.wait_ge(drow_done, n - 3)
                        nc.tensor.matmul(banks[n % 4][:], wrep[:, h, :], h2t[:, g * GW:(g + 1) * GW],
                                         start=True, stop=True).then_inc(drow_ps, 1)
                pe.wait_ge(drow_done, NG * H)
                with pe.Fori(0, NC) as b:
                    for h in range(H):
                        i = b * H + h
                        pe.wait_ge(p_ready, i + 1)
                        for g in range(NG):
                            if g >= 2:
                                pe.wait_ge(p_evac, NG * i + g - 1)
                            for k in range(GB):
                                c = GB * g + k
                                last = nc.tensor.transpose(banks[g % 2][:, k * P:(k + 1) * P], e[:, c * P:(c + 1) * P],
                                                           ident[:])
                            last.then_inc(p_ps, 1)
                        pe.wait_ge(p_evac, NG * (i + 1))
                        for c in range(NC):
                            last = nc.tensor.matmul(banks[2 + h][:, 0:D], pt[:, c * P:(c + 1) * P],
                                                    wh[:, c, h * D:(h + 1) * D], start=(c == 0), stop=(c == NC - 1))
                        last.then_inc(pv, 1)

            @block.scalar
            def _(act):
                for n in range(NG * H):
                    act.wait_ge(drow_ps, n + 1)
                    nc.scalar.copy(drow[:, n // NG, (n % NG) * GW:(n % NG + 1) * GW], banks[n % 4][:]).then_inc(drow_done, 1)
                with act.Fori(0, NC) as b:
                    for h in range(H):
                        i = b * H + h
                        act.wait_ge(e_ready, i + 1)
                        nc.scalar.activation(e[:], e[:], ACT.Exp, bias=nmax[:, 0:1], scale=1.0,
                                             accum_out=den[:, h:h + 1]).then_inc(p_ready, 1)
                        for g in range(NG):
                            act.wait_ge(p_ps, NG * i + g + 1)
                            if h > 0 and g == 0:
                                act.wait_ge(pv, i)
                            nc.scalar.copy(pt[:, g * GW:(g + 1) * GW], banks[g % 2][:]).then_inc(p_evac, 1)
                    act.wait_ge(s_elu, b + 1)
                    nc.scalar.activation(neg[:], neg[:], ACT.Exp).then_inc(elu_exp, 1)

            @block.vector
            def _(vec):
                nc.vector.tensor_copy(wrep[:], w_ext[:, F + H:E].unsqueeze(2).to_broadcast([P, H, P])).then_inc(wrep_ready, 1)
                vec.wait_ge(drow_done, NG * H)
                vec.sem_inc(arow_free, 1)
                with vec.Fori(0, NC) as b:
                    count = [0]

                    def link(ins):
                        count[0] += 1
                        ins.then_inc(vec3, 1)
                        vec.wait_ge(vec3, VL * b + count[0])
                    vec.wait_ge(arow_in, 16 * (b + 1))
                    link(nc.vector.tensor_scalar(keep[:], arow[:], 0.0, None, ALU.is_gt))
                    link(nc.vector.tensor_scalar(fill[:], keep[:], 1.0, NEG_INF, ALU.subtract, ALU.mult))
                    link(nc.vector.tensor_copy(ssrc[:], wh[:, bass.ds(b, 1), F:F + H].rearrange("p o e -> p (o e)")))
                    for h in range(H):
                        i = b * H + h
                        if h > 0:
                            vec.wait_ge(p_evac, NG * i)
                        link(nc.vector.tensor_scalar(e[:], drow[:, h, :], ssrc[:, h:h + 1], None, ALU.add))
                        link(nc.vector.scalar_tensor_tensor(e[:], e[:], ALPHA, e[:], ALU.mult, ALU.max))
                        link(nc.vector.tensor_tensor(e[:], e[:], keep[:], ALU.mult))
                        link(nc.vector.tensor_tensor(e[:], e[:], fill[:], ALU.add))
                        link(nc.vector.tensor_reduce(nmax[:], e[:], AX.X, ALU.max, negate=True))
                        vec.sem_inc(e_ready, 1)
                        vec.wait_ge(p_ready, i + 1)
                        link(nc.vector.reciprocal(rden[:], den[:, h:h + 1]))
                        vec.wait_ge(pv, i + 1)
                        ins = nc.vector.tensor_scalar(o[:, h * D:(h + 1) * D], banks[2 + h][:, 0:D], rden[:, 0:1], None,
                                                      ALU.mult)
                    ins.then_inc(arow_free, 1)
                    vec.wait_ge(arow_free, b + 2)
                    nc.vector.tensor_scalar(neg[:], o[:], 0.0, None, ALU.min).then_inc(s_elu, 1)
                    vec.wait_ge(elu_exp, b + 1)
                    link(nc.vector.tensor_scalar(o[:], o[:], 0.0, None, ALU.max))
                    link(nc.vector.scalar_tensor_tensor(o[:], neg[:], -1.0, o[:], ALU.add, ALU.add))
                    link(nc.vector.tensor_tensor(o[:], o[:], xs[:, bass.ds(b, 1), :].rearrange("p o f -> p (o f)"), ALU.add))
                    vec.sem_inc(o_ready, 1)
                    vec.wait_ge(stored, 16 * (b + 1))


_INS = ["x", "adj", "L1_gnn_W", "L1_gnn_a"]


def kernel(**inputs):
    import numpy as _np
    import concourse.bacc as _bacc
    from concourse import mybir as _mybir
    from concourse.bass_utils import run_bass_kernel_spmd as _run

    nc = _bacc.Bacc("TRN2", target_bir_lowering=False, num_devices=1)
    arrays, args = {}, []
    for name in _INS:
        a = _np.ascontiguousarray(inputs[name])
        arrays[f"in_{name}"] = a
        args.append(nc.dram_tensor(f"in_{name}", a.shape, _mybir.dt.from_np(a.dtype), kind="ExternalInput").ap())
    out = nc.dram_tensor("out_x", inputs["x"].shape, _mybir.dt.float32, kind="ExternalOutput").ap()
    emit(nc, *args, out)
    r = _run(nc, [arrays], core_ids=[0])
    return r.results[0]["out_x"]
```
